# Optimizing a Trainium2 kernel written in Bass

```python
import numpy as np
import jax
import jax.numpy as jnp

def _softmax(x, axis=-1):
    return jax.nn.softmax(x, axis=axis)

def _gelu(x):
    return jax.nn.gelu(x, approximate=True)

def _silu(x):
    return jax.nn.silu(x)

def _sigmoid(x):
    return jax.nn.sigmoid(x)

def _layernorm(x, axis=-1, eps=1e-05):
    m = jnp.mean(x, axis=axis, keepdims=True)
    v = jnp.var(x, axis=axis, keepdims=True)
    return (x - m) / jnp.sqrt(v + eps)

def _scatter_add(tgt, idx, src, axis=0):
    return tgt.at[idx].add(src)

def _segment_sum(src, seg, n):
    return jax.ops.segment_sum(src, seg, n)
kernel_name = 'mk_seq_preln_d2_jaxref_r8_4b976f'

def setup_inputs(seed: int=0):
    np.random.seed(seed)
    _w = jnp.asarray

    def _L0_attn_setup():
        import jax, jax.numpy as jnp
        import numpy as np
        D_MODEL = 256
        N_HEADS = 16
        HEAD_DIM = D_MODEL // N_HEADS

        def _alibi_slopes(n_heads: int) -> jnp.ndarray:
            start = 2.0 ** (-8.0 / n_heads)
            return jnp.asarray([start * start ** i for i in range(n_heads)], dtype=jnp.float32)
        key = jax.random.key(seed)
        ks = jax.random.split(key, 9)
        B, S, D = (2, 256, D_MODEL)
        scale = 1.0 / np.sqrt(D)
        return {'x': jax.random.normal(ks[0], (B, S, D), dtype=jnp.float32), 'wq': jax.random.normal(ks[1], (D, D), dtype=jnp.float32) * scale, 'bq': jnp.zeros((D,), dtype=jnp.float32), 'wk': jax.random.normal(ks[2], (D, D), dtype=jnp.float32) * scale, 'bk': jnp.zeros((D,), dtype=jnp.float32), 'wv': jax.random.normal(ks[3], (D, D), dtype=jnp.float32) * scale, 'bv': jnp.zeros((D,), dtype=jnp.float32), 'wo': jax.random.normal(ks[4], (D, D), dtype=jnp.float32) * scale, 'bo': jnp.zeros((D,), dtype=jnp.float32)}
    _L0_attn_in = _L0_attn_setup()

    def _L0_ffn_setup():
        import jax, jax.numpy as jnp
        import numpy as np
        DIM = 256
        INTER = 176
        N_EXPERTS = 16
        TOP_K = 2
        N_SHARED = 2
        SHARED_INTER = N_SHARED * INTER

        def _swiglu(t, wa, wb, wo):
            h = jax.nn.silu(t @ wa.T) * (t @ wb.T)
            return h @ wo.T
        key = jax.random.key(seed)
        ks = jax.random.split(key, 9)
        s = 0.02
        return {'x': jax.random.normal(ks[0], (4, 256, DIM), dtype=jnp.float32), 'gate_w': jax.random.normal(ks[1], (N_EXPERTS, DIM), dtype=jnp.float32) * s, 'w1': jax.random.normal(ks[2], (N_EXPERTS, INTER, DIM), dtype=jnp.float32) * s, 'w2': jax.random.normal(ks[3], (N_EXPERTS, DIM, INTER), dtype=jnp.float32) * s, 'w3': jax.random.normal(ks[4], (N_EXPERTS, INTER, DIM), dtype=jnp.float32) * s, 'sw1': jax.random.normal(ks[5], (SHARED_INTER, DIM), dtype=jnp.float32) * s, 'sw2': jax.random.normal(ks[6], (DIM, SHARED_INTER), dtype=jnp.float32) * s, 'sw3': jax.random.normal(ks[7], (SHARED_INTER, DIM), dtype=jnp.float32) * s}
    _L0_ffn_in = _L0_ffn_setup()

    def _L1_attn_setup():
        import jax, jax.numpy as jnp
        import numpy as np
        import math
        HID = 256
        NH = 16
        NKV = 4
        NG = NH // NKV
        LORA = 64
        D_ROPE = 64
        D_NOPE = 128
        D_V = 128
        D_QK = D_NOPE + D_ROPE
        B, S = (2, 256)
        ROPE_BASE = 10000.0

        def _rope(x, seq_len):
            inv_freq = 1.0 / ROPE_BASE ** (jnp.arange(0, D_ROPE, 2, dtype=jnp.float32) / D_ROPE)
            t = jnp.arange(seq_len, dtype=jnp.float32)
            freqs = jnp.outer(t, inv_freq)
            emb = jnp.concatenate([freqs, freqs], axis=-1)
            cos = jnp.cos(emb)[None, :, None, :].astype(x.dtype)
            sin = jnp.sin(emb)[None, :, None, :].astype(x.dtype)
            x1, x2 = jnp.split(x, 2, axis=-1)
            rot = jnp.concatenate([-x2, x1], axis=-1)
            return x * cos + rot * sin
        key = jax.random.key(seed)
        ks = jax.random.split(key, 5)
        s = lambda fan_in: 1.0 / math.sqrt(fan_in)
        return {'hidden_states': jax.random.normal(ks[0], (B, S, HID), jnp.float32), 'Wqkv': jax.random.uniform(ks[1], (HID, NH * D_QK + LORA), jnp.float32, -s(HID), s(HID)), 'Wk_up': jax.random.uniform(ks[2], (LORA, NKV * D_QK), jnp.float32, -s(LORA), s(LORA)), 'Wv_up': jax.random.uniform(ks[3], (LORA, NKV * D_V), jnp.float32, -s(LORA), s(LORA)), 'Wo': jax.random.uniform(ks[4], (NH * D_V, HID), jnp.float32, -s(NH * D_V), s(NH * D_V))}
    _L1_attn_in = _L1_attn_setup()

    def _L1_ffn_setup():
        import jax, jax.numpy as jnp
        import numpy as np
        DIM = 256
        INTER = 176
        N_EXPERTS = 16
        TOP_K = 2
        N_SHARED = 2
        SHARED_INTER = N_SHARED * INTER

        def _swiglu(t, wa, wb, wo):
            h = jax.nn.silu(t @ wa.T) * (t @ wb.T)
            return h @ wo.T
        key = jax.random.key(seed)
        ks = jax.random.split(key, 9)
        s = 0.02
        return {'x': jax.random.normal(ks[0], (4, 256, DIM), dtype=jnp.float32), 'gate_w': jax.random.normal(ks[1], (N_EXPERTS, DIM), dtype=jnp.float32) * s, 'w1': jax.random.normal(ks[2], (N_EXPERTS, INTER, DIM), dtype=jnp.float32) * s, 'w2': jax.random.normal(ks[3], (N_EXPERTS, DIM, INTER), dtype=jnp.float32) * s, 'w3': jax.random.normal(ks[4], (N_EXPERTS, INTER, DIM), dtype=jnp.float32) * s, 'sw1': jax.random.normal(ks[5], (SHARED_INTER, DIM), dtype=jnp.float32) * s, 'sw2': jax.random.normal(ks[6], (DIM, SHARED_INTER), dtype=jnp.float32) * s, 'sw3': jax.random.normal(ks[7], (SHARED_INTER, DIM), dtype=jnp.float32) * s}
    _L1_ffn_in = _L1_ffn_setup()
    _d = {'L0_attn_x': _L0_attn_in['x'], 'L0_attn_wq': _L0_attn_in['wq'], 'L0_attn_bq': _L0_attn_in['bq'], 'L0_attn_wk': _L0_attn_in['wk'], 'L0_attn_bk': _L0_attn_in['bk'], 'L0_attn_wv': _L0_attn_in['wv'], 'L0_attn_bv': _L0_attn_in['bv'], 'L0_attn_wo': _L0_attn_in['wo'], 'L0_attn_bo': _L0_attn_in['bo'], 'L0_ffn_gate_w': _L0_ffn_in['gate_w'], 'L0_ffn_w1': _L0_ffn_in['w1'], 'L0_ffn_w2': _L0_ffn_in['w2'], 'L0_ffn_w3': _L0_ffn_in['w3'], 'L0_ffn_sw1': _L0_ffn_in['sw1'], 'L0_ffn_sw2': _L0_ffn_in['sw2'], 'L0_ffn_sw3': _L0_ffn_in['sw3'], 'L1_attn_Wqkv': _L1_attn_in['Wqkv'], 'L1_attn_Wk_up': _L1_attn_in['Wk_up'], 'L1_attn_Wv_up': _L1_attn_in['Wv_up'], 'L1_attn_Wo': _L1_attn_in['Wo'], 'L1_ffn_gate_w': _L1_ffn_in['gate_w'], 'L1_ffn_w1': _L1_ffn_in['w1'], 'L1_ffn_w2': _L1_ffn_in['w2'], 'L1_ffn_w3': _L1_ffn_in['w3'], 'L1_ffn_sw1': _L1_ffn_in['sw1'], 'L1_ffn_sw2': _L1_ffn_in['sw2'], 'L1_ffn_sw3': _L1_ffn_in['sw3']}
    _x0 = _d['L0_attn_x']
    _d['L0_attn_x'] = jax.random.normal(jax.random.fold_in(jax.random.key(seed), 1), (2, 1024, 256), dtype=_x0.dtype)
    del _x0
    return _d

def reference(L0_attn_x, L0_attn_wq, L0_attn_bq, L0_attn_wk, L0_attn_bk, L0_attn_wv, L0_attn_bv, L0_attn_wo, L0_attn_bo, L0_ffn_gate_w, L0_ffn_w1, L0_ffn_w2, L0_ffn_w3, L0_ffn_sw1, L0_ffn_sw2, L0_ffn_sw3, L1_attn_Wqkv, L1_attn_Wk_up, L1_attn_Wv_up, L1_attn_Wo, L1_ffn_gate_w, L1_ffn_w1, L1_ffn_w2, L1_ffn_w3, L1_ffn_sw1, L1_ffn_sw2, L1_ffn_sw3):

    def _L0_attn_ref(x, wq, bq, wk, bk, wv, bv, wo, bo):
        import jax, jax.numpy as jnp
        import numpy as np
        D_MODEL = 256
        N_HEADS = 16
        HEAD_DIM = D_MODEL // N_HEADS

        def _alibi_slopes(n_heads: int) -> jnp.ndarray:
            start = 2.0 ** (-8.0 / n_heads)
            return jnp.asarray([start * start ** i for i in range(n_heads)], dtype=jnp.float32)
        B, S, D = x.shape
        H, hd = (N_HEADS, HEAD_DIM)

        def heads(y):
            return y.reshape(B, S, H, hd).transpose(0, 2, 1, 3)
        q = heads(x @ wq + bq)
        k = heads(x @ wk + bk)
        v = heads(x @ wv + bv)
        scores = jnp.einsum('bhqd,bhkd->bhqk', q, k) / jnp.sqrt(jnp.float32(hd))
        pos = jnp.arange(S)
        rel = pos[None, :] - pos[:, None]
        slopes = _alibi_slopes(H)
        bias = slopes[:, None, None] * rel.astype(jnp.float32)
        causal = jnp.where(rel > 0, -jnp.inf, 0.0).astype(jnp.float32)
        scores = scores + (bias + causal)[None]
        attn = jax.nn.softmax(scores, axis=-1)
        out = jnp.einsum('bhqk,bhkd->bhqd', attn, v)
        out = out.transpose(0, 2, 1, 3).reshape(B, S, D)
        return out @ wo + bo

    def _L0_ffn_ref(x, gate_w, w1, w2, w3, sw1, sw2, sw3):
        import jax, jax.numpy as jnp
        import numpy as np
        DIM = 256
        INTER = 176
        N_EXPERTS = 16
        TOP_K = 2
        N_SHARED = 2
        SHARED_INTER = N_SHARED * INTER

        def _swiglu(t, wa, wb, wo):
            h = jax.nn.silu(t @ wa.T) * (t @ wb.T)
            return h @ wo.T
        shape = x.shape
        t = x.reshape(-1, DIM)
        scores = jax.nn.softmax(t @ gate_w.T, axis=-1)
        weights, indices = jax.lax.top_k(scores, TOP_K)
        y = jnp.zeros_like(t)
        for e in range(N_EXPERTS):
            w_e = jnp.sum(jnp.where(indices == e, weights, 0.0), axis=-1)
            y = y + _swiglu(t, w1[e], w3[e], w2[e]) * w_e[:, None]
        z = _swiglu(t, sw1, sw3, sw2)
        return (y + z).reshape(shape)

    def _L1_attn_ref(hidden_states, Wqkv, Wk_up, Wv_up, Wo):
        import jax, jax.numpy as jnp
        import numpy as np
        import math
        HID = 256
        NH = 16
        NKV = 4
        NG = NH // NKV
        LORA = 64
        D_ROPE = 64
        D_NOPE = 128
        D_V = 128
        D_QK = D_NOPE + D_ROPE
        B, S = (2, 256)
        ROPE_BASE = 10000.0

        def _rope(x, seq_len):
            inv_freq = 1.0 / ROPE_BASE ** (jnp.arange(0, D_ROPE, 2, dtype=jnp.float32) / D_ROPE)
            t = jnp.arange(seq_len, dtype=jnp.float32)
            freqs = jnp.outer(t, inv_freq)
            emb = jnp.concatenate([freqs, freqs], axis=-1)
            cos = jnp.cos(emb)[None, :, None, :].astype(x.dtype)
            sin = jnp.sin(emb)[None, :, None, :].astype(x.dtype)
            x1, x2 = jnp.split(x, 2, axis=-1)
            rot = jnp.concatenate([-x2, x1], axis=-1)
            return x * cos + rot * sin
        b, s, _ = hidden_states.shape
        qkv = hidden_states @ Wqkv
        q, c_kv = jnp.split(qkv, [NH * D_QK], axis=-1)
        q = q.reshape(b, s, NH, D_QK)
        k = (c_kv @ Wk_up).reshape(b, s, NKV, D_QK)
        v = (c_kv @ Wv_up).reshape(b, s, NKV, D_V)
        q_nope, q_rope = jnp.split(q, [D_NOPE], axis=-1)
        k_nope, k_rope = jnp.split(k, [D_NOPE], axis=-1)
        q = jnp.concatenate([q_nope, _rope(q_rope, s)], axis=-1)
        k = jnp.concatenate([k_nope, _rope(k_rope, s)], axis=-1)
        k = jnp.repeat(k, NG, axis=2)
        v = jnp.repeat(v, NG, axis=2)
        scale = 1.0 / math.sqrt(D_QK)
        scores = jnp.einsum('bqhd,bkhd->bhqk', q, k) * scale
        causal = jnp.tril(jnp.ones((s, s), bool))
        scores = jnp.where(causal[None, None], scores, jnp.finfo(scores.dtype).min)
        probs = jax.nn.softmax(scores, axis=-1)
        out = jnp.einsum('bhqk,bkhd->bqhd', probs, v).reshape(b, s, NH * D_V)
        return out @ Wo

    def _L1_ffn_ref(x, gate_w, w1, w2, w3, sw1, sw2, sw3):
        import jax, jax.numpy as jnp
        import numpy as np
        DIM = 256
        INTER = 176
        N_EXPERTS = 16
        TOP_K = 2
        N_SHARED = 2
        SHARED_INTER = N_SHARED * INTER

        def _swiglu(t, wa, wb, wo):
            h = jax.nn.silu(t @ wa.T) * (t @ wb.T)
            return h @ wo.T
        shape = x.shape
        t = x.reshape(-1, DIM)
        scores = jax.nn.softmax(t @ gate_w.T, axis=-1)
        weights, indices = jax.lax.top_k(scores, TOP_K)
        y = jnp.zeros_like(t)
        for e in range(N_EXPERTS):
            w_e = jnp.sum(jnp.where(indices == e, weights, 0.0), axis=-1)
            y = y + _swiglu(t, w1[e], w3[e], w2[e]) * w_e[:, None]
        z = _swiglu(t, sw1, sw3, sw2)
        return (y + z).reshape(shape)
    x = L0_attn_x
    x = x + _L0_attn_ref(_layernorm(x, axis=-1), L0_attn_wq, L0_attn_bq, L0_attn_wk, L0_attn_bk, L0_attn_wv, L0_attn_bv, L0_attn_wo, L0_attn_bo)
    x = x + _L0_ffn_ref(_layernorm(x, axis=-1), L0_ffn_gate_w, L0_ffn_w1, L0_ffn_w2, L0_ffn_w3, L0_ffn_sw1, L0_ffn_sw2, L0_ffn_sw3)
    x = x + _L1_attn_ref(_layernorm(x, axis=-1), L1_attn_Wqkv, L1_attn_Wk_up, L1_attn_Wv_up, L1_attn_Wo)
    x = x + _L1_ffn_ref(_layernorm(x, axis=-1), L1_ffn_gate_w, L1_ffn_w1, L1_ffn_w2, L1_ffn_w3, L1_ffn_sw1, L1_ffn_sw2, L1_ffn_sw3)
    return x

_drawn_inputs = setup_inputs


def setup_inputs(seed=0):
    import zlib

    import numpy as np

    out = dict(_drawn_inputs(seed))
    spreads = {'L0_attn_bq': (0.0, 0.362),
     'L0_attn_bk': (0.0, 0.8),
     'L0_attn_bv': (0.0, 0.1),
     'L0_attn_bo': (0.0, 0.1)}
    factors = {'L0_ffn_gate_w': 8.0,
     'L0_ffn_w1': 8.0,
     'L0_ffn_w2': 8.0,
     'L0_ffn_w3': 8.0,
     'L0_ffn_sw1': 3.08,
     'L0_ffn_sw2': 3.052,
     'L0_ffn_sw3': 3.036,
     'L1_attn_Wk_up': 8.0,
     'L1_ffn_gate_w': 8.0,
     'L1_ffn_w1': 8.0,
     'L1_ffn_w2': 8.0,
     'L1_ffn_w3': 8.0,
     'L1_ffn_sw1': 3.082,
     'L1_ffn_sw2': 3.052,
     'L1_ffn_sw3': 3.035}
    for name, (base, spread) in spreads.items():
        noise = np.random.default_rng([zlib.crc32(name.encode()), seed]).standard_normal(out[name].shape)
        drawn = base * np.exp(spread * noise) if base else spread * noise
        out[name] = jnp.asarray(drawn.astype(out[name].dtype))
    for name, factor in factors.items():
        out[name] = (out[name] * factor).astype(out[name].dtype)
    return out
```

```python
from contextlib import ExitStack

import numpy as np
import concourse.bass as bass
from concourse import mybir

F32 = mybir.dt.float32
F32R = mybir.dt.float32r
BF16 = mybir.dt.bfloat16
I32 = mybir.dt.int32
U32 = mybir.dt.uint32
ALU = mybir.AluOpType
ACT = mybir.ActivationFunctionType
AXX = mybir.AxisListType.X

P = 128
D = 256
KC = D // P
BATCH = 2
SEQ = 1024
T = BATCH * SEQ
NT = T // P
TB = SEQ // P
QC = 512
EPS = 1e-5
MASKED = -1e30
COUNT_AT = 5
SBUF = 229376

UNITS = [(0, kt) for kt in range(4)] + [(1, kt) for kt in range(8)]
GROUPS = [g for h in range(4) for g in
          ([(h, 0, 0), (h, 1, QC)], [(h, 2, 0), (h, 3, QC)], *([(h, qt, 0)] for qt in range(4, 8)))]


def first_query(qc, kt):
    return max(0, kt * P - qc * QC)


def tables():
    t = np.arange(SEQ, dtype=np.float32)
    start = 2.0 ** (-8.0 / 16)
    slopes = np.asarray([start * start ** i for i in range(16)], np.float32)
    four = slopes * np.float32(4)
    hi = (four.view(np.uint32) & np.uint32(0xFFFFF000)).view(np.float32)
    lo = four - hi
    coef = np.zeros((P, 4, 4), np.float32)
    for g in range(4):
        for h in range(4):
            a, b, r = hi[4 * g + h], lo[4 * g + h], 32 * h + 16
            coef[r, g] = (0, -a, 1, 0)
            coef[r + 1, g] = (1, 0, 0, a)
            coef[r + 2, g] = (0, -b, 1, 0)
            coef[r + 3, g] = (b, 0, 0, 1)
            coef[r + 4, g] = (0, 0, 1, 0)
    inv = (np.float32(1) / np.power(np.float32(10000), np.arange(0, 64, 2, dtype=np.float32) / np.float32(64)))
    ang = np.outer(inv.astype(np.float32), t).astype(np.float32)
    rope = np.zeros((P, 2, SEQ), np.float32)
    rope[64:96, 0] = rope[96:128, 0] = np.cos(ang)
    rope[64:96, 1] = np.sin(ang)
    rope[96:128, 1] = -np.sin(ang)
    i = np.arange(P)
    masks = np.full((P, 3, P), MASKED, np.float32)
    masks[:, 0] = np.where(i[None, :] > i[:, None], MASKED, 0)
    masks[:, 1] = np.where(i[:, None] > i[None, :], MASKED, 0)
    spread = np.zeros((P, P), np.float32)
    for h in range(4):
        spread[32 * h + 16, 32 * h:32 * h + 32] = 1
    before = (i[:, None] < i[None, :]).astype(np.float32)
    e = np.arange(16, dtype=np.float32)
    small = np.zeros((1, 16 + 16 * 16 + NTILE * 16), np.float32)
    small[:, 0:16] = 16 - e
    small[:, 16:272] = (e[None, :] < e[:, None]).astype(np.float32).reshape(1, 256)
    small[:, 272:] = np.repeat(np.arange(NTILE, dtype=np.float32), 16)[None]
    return {
        "c_sel": np.repeat((np.arange(P)[:, None] % 4 == np.arange(4)[None]) & (np.arange(P)[:, None] < 8), P, 1).reshape(P, 4, P).astype(np.float32),
        "c_ident": np.eye(P, dtype=np.float32), "c_masks": masks, "c_spread": spread, "c_before": before,
        "c_pos": t.reshape(1, SEQ), "c_coef": coef, "c_rope": rope, "c_small": small,
    }


SCALE1 = float(1.0 / np.sqrt(192.0))
NTILE = 48
NE = 18
HID = 176
HH = HID // 2
NSH = 2 * NT


class Count:

    def __init__(self, sem):
        self.sem, self.n = sem, 0

    def up(self, ins):
        self.n += 1
        ins.then_inc(self.sem, 1)
        return self.n


def build(nc, **A):
    ctx = ExitStack()
    with ctx:
        def sb(name, shape, dt=F32):
            return ctx.enter_context(nc.sbuf_tensor(name, shape, dt))

        def sem(name):
            return ctx.enter_context(nc.semaphore(name))

        X = sb("X", [P, NT, D])
        XT = sb("XT", [P, KC, T])
        stats = sb("stats", [P, NT, 6])
        mv = sb("mv", [P, NT, 2])
        rs = sb("rs", [P, 4, NT])
        ident = sb("ident", [P, P])
        identb = sb("identb", [P, P], BF16)
        masks = sb("masks", [P, 3, P], BF16)
        spread = sb("spread", [P, P])
        coef = sb("coef", [P, 4, 4])
        bqk = sb("bqk", [P, 4, 2])
        cg = sb("cg", [P, 2, 4])
        before = sb("before", [P, P])
        ones = sb("ones", [P, P])
        small = sb("small", [P, 16 + 256 + NTILE * 16])
        zeros = sb("zeros", [P, D])
        arena = nc.sbuf_base

        class Phase:

            def __init__(self):
                self.at = arena + 64 - arena % 64

            def __call__(self, name, shape, dt=F32):
                size = int(np.prod(shape[1:])) * (2 if dt == BF16 else 4)
                assert self.at + size <= SBUF, (name, self.at + size)
                t = nc.alloc_sbuf_tensor_at(name, shape, dt, offset=self.at)
                self.at += (size + 63) // 64 * 64
                return t

        XN = Phase()("XN", [P, NT, D])
        arena += NT * D * 4
        ph = Phase()
        wqk = ph("wqk", [P, 4, P])
        wo0 = ph("wo0", [P, 4, D])
        wv = ph("wv", [P, KC, D])
        bob = ph("bob", [P, D])
        bvb = ph("bvb", [P, D])
        pos = ph("pos", [P, SEQ])
        masksf = ph("masksf", [P, 3, P])
        V = ph("V", [P, NT, D])
        VS = ph("VS", [P, 2, TB, 4, 32])
        tq = ph("tq", [P, 2, QC])
        QKs = ph("QKs", [P, 4, SEQ], F32R)
        QS = ph("QS", [P, 2, 4, SEQ], F32R)
        KS = ph("KS", [P, 2, 4, SEQ], F32R)
        PT = ph("PT", [P, 3, 2, QC])
        MX = ph("MX", [P, 2, P])
        mneg = ph("mneg", [32, P])
        mh = ph("mh", [32, 2, P], F32R)
        oT = ph("oT", [P, QC])
        rc = ph("rc", [P, 16])
        rb = ph("rb", [P, 16, 32])
        oN = ph("oN", [P, QC])

        pa = Phase()
        pa.at -= NT * D * 4
        KH = pa("KH", [P, 2, SEQ], F32R)
        KL = pa("KL", [P, 2, SEQ], F32R)
        cT = pa("cT", [64, T])
        CA = pa("CA", [P, NT, 65])
        wc = pa("wc", [P, KC, 64])
        wqn = pa("wqn", [P, 4, D])
        wkT = pa("wkT", [P, 64])
        WQ = pa("WQ", [P, 4, KC, P])
        WK = pa("WK", [64, P])
        wog = pa("wog", [P, 4, D])
        wvT = pa("wvT", [P, 64])
        WVO = pa("WVO", [P, 2, D])
        rope = pa("rope", [P, 2, SEQ])
        selb = pa("selb", [P, 4, P], BF16)
        MR = pa("MR", [P, 2, SEQ], BF16)
        QH = pa("QH", [P, 2, 4, SEQ], F32R)
        QL = pa("QL", [P, 2, 4, SEQ], F32R)
        r1 = pa("r1", [P, 2, QC])
        r2 = pa("r2", [P, 2, QC])
        F = pa("F", [P, 2, QC])
        PT1 = pa("PT1", [P, 4, QC])
        rc1 = pa("rc1", [P, 2, 4])
        rt1 = pa("rt1", [P, 1])
        oq1 = pa("oq1", [P, 2, TB, 2, 64])
        MX1 = pa("MX1", [P, 2, P])
        mn1 = pa("mn1", [32, 2, P])
        mb1 = pa("mb1", [32, 2, P], BF16)
        oN1_at = pa.at
        oN1 = pa("oN1", [P, 2, SEQ])
        pa.at = oN1_at
        self_ = pa("self_", [P, 4, P])
        pm = Phase()
        W13 = pm("W13", [P, KC, NE, 2 * HID])
        W2 = pm("W2", [HH, 2, NE, D])
        gw = pm("gw", [P, KC, 16])
        xs = pm("xs", [P, 4, D])
        xTs = pm("xTs", [P, 2, KC, P])
        sg = pm("sg", [P, 2, HID])
        hb = pm("hb", [P, 2, HID])
        hT = pm("hT", [HH, 2, 2, P])
        ys = pm("ys", [P, 2, D])
        yg = pm("yg", [P, 4, 2, D])
        R = pm("R", [P, 8, NT, 16])
        rt = pm("rt", [P, 8, NT])
        carry = pm("carry", [P, NT + 1, 16])
        tl = pm("tl", [P, 4, 16])
        tli = pm("tli", [P, 16], I32)
        owner = pm("owner", [P, NTILE, 16])
        lt = pm("lt", [P, 16, 16])
        eidf = pm("eidf", [P, NTILE])
        eid = pm("eid", [P, NTILE], I32)
        slot = pm("slot", [P, 2, NT], U32)
        slots = nc.dram_tensor("slots", [NTILE * P, D], F32, kind="Internal").ap()
        outs = nc.dram_tensor("outs", [NTILE * P, D], F32, kind="Internal").ap()
        PS = ctx.enter_context(nc.psum_tensor("PS", [P, 8, QC], F32))
        psM = PS[:, 4:6, :].rearrange("p a b -> p (a b)")
        psO = PS[:, 6, :]
        psX = PS[:, 7, :]

        const_in = sem("const_in"); x_in = sem("x_in"); w_in = sem("w_in")
        consts_made = sem("consts_made")
        dve_done = sem("dve_done")
        dv = Count(dve_done)
        out_done = sem("out_done")
        pool_ready = sem("pool_ready")
        LN = [{k: sem(f"ln{n}_{k}") for k in ("var", "sd", "xn", "t", "xt")} for n in range(4)]
        v_ready = sem("v_ready"); v_taken = sem("v_taken"); bo_added = sem("bo_added")
        coef_ready = sem("coef_ready")
        a0 = {k: sem("a0_" + k) for k in (
            "scores", "probs", "pv", "max_scored", "max_taken", "x_ready", "x_used", "hi_ready",
            "split", "neg", "neg_hi", "evac", "normed", "staged", "w_in", "row0", "row1", "recip", "cg")}
        copied = [[sem(f"a0_copied{p}{h}") for h in range(4)] for p in range(2)]

        moe = [{k: sem(f"m{n}_{k}") for k in (
            "w_in", "gate_in", "shared_in", "logits", "shifted", "exps", "onehot", "counted", "eid", "slot", "scattered",
            "u", "sg", "h", "ht", "hT", "d", "y", "t", "xT", "xs0", "xs1", "xs2", "xs3", "stored0", "stored1",
            "got0", "got1", "got2", "got3", "added")} for n in range(2)]
        a1 = {k: sem("a1_" + k) for k in (
            "scores", "probs", "pv", "max_scored", "max_taken", "x_ready", "x_used", "plain", "roped", "summed", "hi_ready",
            "split", "neg", "neg_mid", "evac", "recip", "w_in", "wt_in", "row0", "row1", "made", "sel", "c_ready", "cT", "ct_turned", "CA")}
        zero_made = sem("zero_made"); zero_in = sem("zero_in")
        block = ctx.enter_context(nc.Block())

        FRONT = ["P0", "P1", "P2", "P3"]
        PREV = ["S1", "B1", "W1a", "W1b"]
        OWN = ["S0", "B0", "W0a", "W0b"]
        ORDERS = {"front": FRONT + ["T"], 0: FRONT + OWN + ["T"], 1: FRONT + PREV + OWN + ["T"], 7: PREV + OWN, "end": PREV}

        def x_index(n, use, kind):
            at = ORDERS[kind].index(use)
            if kind == "front":
                return at
            if kind == 0:
                return 5 + at
            base = 14
            if kind == 1:
                return (n - 1) * 13 + (base + at)
            return base + 6 * 13 + at + (8 if kind == "end" else 0)

        CHUNKS = ["K0", "K1", "Q00", "Q01", "Q10", "Q11", "Q20", "Q21", "Q30", "Q31"]
        X1_AT = {s: [] for s in range(48)}
        for at, use in ((0, "K0"), (1, "K1"), (2, "A"), (2, "Q00"), (4, "N3"), (5, "Q01"), (6, "O0"), (7, "O1"), (8, "O2"), (9, "O3"),
                        (11, "Q10"), (13, "Q11"), (16, "Q20"), (18, "Q21"), (20, "Q30"), (22, "Q31"), (24, "V"), (28, "N0"),
                        (30, "N1"), (45, "N2")):
            X1_AT[at].append(use)
        MAX1_AT = [[] for _ in range(48)]
        for i in range(len(GROUPS)):
            MAX1_AT[10 + i * 36 // len(GROUPS)].append(i)
        HI_AT = {}
        for s in range(48):
            for use in X1_AT[s]:
                if use in CHUNKS:
                    HI_AT.setdefault(s + 2 if use not in ("K0", "K1") else s + 1, []).append(use)
        SLOTS1 = [(h, qc, kt) for h in range(4) for qc, kt in UNITS]
        PREV1 = ["N3", "O0", "O1", "O2", "O3"]
        ALL1 = [u for s in range(48) for u in X1_AT[s]]
        FRONT1 = ["A"] + CHUNKS

        def has1(use, kind):
            if kind == "end":
                return use in PREV1
            if use in PREV1:
                return kind != 0
            if use in CHUNKS:
                return kind != 7
            if use == "A":
                return kind == "odd"
            if use == "V":
                return kind in (0, "even")
            return True

        ORDERS1 = {kind: [u for u in ALL1 if has1(u, kind)] + (["T"] if kind != 7 else []) for kind in (0, "odd", "even", 7)}
        ORDERS1["front"] = FRONT1 + ["T"]
        ORDERS1["end"] = PREV1
        FULL1 = len(ORDERS1["odd"])
        BASE1 = len(ORDERS1["front"]) + len(ORDERS1[0])
        assert FULL1 == len(ORDERS1["even"])

        def x1_index(n, use, kind):
            at = ORDERS1[kind].index(use)
            if kind == "front":
                return at
            if kind == 0:
                return len(ORDERS1["front"]) + at
            if kind in ("odd", "even"):
                return (n - 1) * FULL1 + (BASE1 + at)
            return BASE1 + 6 * FULL1 + at + (len(ORDERS1[7]) if kind == "end" else 0)


        X_AT = {0: "P0", 1: "P1", 2: "P2", 3: "P3", 4: "S1", 5: "B1", 6: "W1a", 7: "W1b", 12: "S0", 13: "B0", 14: "W0a", 15: "W0b"}
        MAX_AT = [[] for _ in range(24)]
        for i in range(len(GROUPS)):
            MAX_AT[7 + i * 16 // len(GROUPS)].append(i)
        SLOTS = [(qc, kt, pair) for qc, kt in UNITS for pair in range(2)]

        @block.sync
        def _(sp):
            for i in range(4):
                sp.dma_start(X[:, 4 * i:4 * i + 4, :], A["x"].rearrange("(t p) d -> p t d", p=P)[:, 4 * i:4 * i + 4, :]).then_inc(x_in, 16)
            sp.dma_start(ident[:], A["c_ident"]).then_inc(const_in, 16)
            sp.dma_start(masksf[:], A["c_masks"]).then_inc(const_in, 16)
            sp.dma_start(spread[:], A["c_spread"]).then_inc(const_in, 16)
            sp.dma_start(coef[:], A["c_coef"]).then_inc(const_in, 16)
            sp.dma_start(bqk[:], A["bqk"]).then_inc(const_in, 16)
            sp.dma_start(pos[:], A["c_pos"].to_broadcast([P, SEQ])).then_inc(const_in, 16)
            sp.dma_start(before[:], A["c_before"]).then_inc(const_in, 16)
            sp.dma_start(small[:], A["c_small"].to_broadcast([P, 16 + 256 + NTILE * 16])).then_inc(const_in, 16)
            sp.dma_start(bvb[:], A["bv"].to_broadcast([P, D])).then_inc(w_in, 16)
            sp.dma_start(bob[:], A["bo"].to_broadcast([P, D])).then_inc(w_in, 16)
            sp.dma_start(wv[:], A["wv"].rearrange("(c p) n -> p c n", p=P)).then_inc(w_in, 16)
            sp.dma_start(wo0[:], A["wo0"].rearrange("g p n -> p g n")).then_inc(w_in, 16)
            sp.dma_start(wqk[:], A["wqk"][0]).then_inc(a0["w_in"], 16)

            def stack(n, par):
                sp.wait_ge(a0["split"], 4 * (n + 1))
                for h in range(4):
                    r = slice(32 * h, 32 * h + 32)
                    for dst, src in ((QS, (0, 0, 1, 1)), (KS, (2, 3, 2, 3))):
                        for quarter in range(4):
                            sp.dma_start(dst[32 * quarter:32 * quarter + 32, par, h, :].bitcast(F32), QKs[r, src[quarter], :].bitcast(F32)).then_inc(copied[par][h], 16)

            def neg_rows(n, par):
                sp.wait_ge(a0["neg"], n + 1)
                for part in range(2):
                    sp.dma_start(QS[20 + 64 * part:21 + 64 * part, par, :, :].rearrange("o h t -> o (h t)").bitcast(F32), mh[:, part, :].bitcast(F32)).then_inc(a0[f"row{par}"], 16)

            stack(0, 0)
            neg_rows(0, 0)
            stack(1, 1)
            sp.wait_ge(a0["x_ready"], x_index(0, "P3", 0) + 1)
            sp.dma_start(wqk[:], A["wqk"][1]).then_inc(a0["w_in"], 16)
            neg_rows(1, 1)
            with sp.Fori(0, 3) as k:
                stack(2 * k + 2, 0)
                neg_rows(2 * k + 2, 0)
                stack(2 * k + 3, 1)
                g = sp.snap(k + 2)
                sp.wait_ge(a0["x_ready"], x_index(2 * k + 2, "P3", 1) + 1)
                sp.dma_start(wqk[:], A["wqk"][bass.ds(g, 1)].rearrange("a p b c -> p (a b) c")).then_inc(a0["w_in"], 16)
                neg_rows(2 * k + 3, 1)
            sp.wait_ge(a0["w_in"], 16 * 5)
            sp.wait_ge(zero_made, 1)
            sp.dma_start(slots.rearrange("(g p) d -> p g d", p=P), zeros[:, None, :].to_broadcast([P, NTILE, D])).then_inc(zero_in, 16)

            def experts(m, layer):
                sp.dma_start(gw[:], A["gw"][layer]).then_inc(m["gate_in"], 16)
                for kc in range(KC):
                    sp.dma_start(W13[:, kc, 16:18], A["w13"][layer, :, kc, 16:18]).then_inc(m["shared_in"], 16)
                sp.dma_start(W2[:, :, 16:18], A["w2"][layer, :, :, 16:18]).then_inc(m["shared_in"], 16)
                for kc in range(KC):
                    sp.dma_start(W13[:, kc, 0:16], A["w13"][layer, :, kc, 0:16]).then_inc(m["w_in"], 16)
                sp.dma_start(W2[:, :, 0:16], A["w2"][layer, :, :, 0:16]).then_inc(m["w_in"], 16)

                def load(g, j):
                    if not isinstance(g, int):
                        sp.wait_ge(m["t"], g - 3)
                    src = slots.rearrange("(g p) d -> p g d", p=P)
                    src = src[:, g:g + 1, :] if isinstance(g, int) else src[:, bass.ds(g, 1), :]
                    sp.dma_start(xs[:, j:j + 1, :], src).then_inc(m[f"xs{j}"], 16)

                def store(g, j):
                    sp.wait_ge(m["y"], NSH + g + 1)
                    dst = outs.rearrange("(g p) d -> p g d", p=P)
                    dst = dst[:, g:g + 1, :] if isinstance(g, int) else dst[:, bass.ds(g, 1), :]
                    sp.dma_start(dst, ys[:, j:j + 1, :]).then_inc(m[f"stored{j}"], 16)

                sp.wait_ge(m["scattered"], 16 * 2 * NT)
                for g in range(4):
                    load(g, g)
                with sp.Fori(0, NTILE // 4 - 1) as k:
                    for j in range(4):
                        load(4 * k + 4 + j, j)
                        store(4 * k + j, j % 2)
                for j in range(4):
                    store(NTILE - 4 + j, j % 2)

            sp.wait_ge(a0["x_used"], x_index(8, "W1b", "end") + 1)
            def attention1():
                def group_weights(g):
                    pick = (lambda name: A[name][g]) if isinstance(g, int) else (lambda name: A[name][bass.ds(g, 1)].rearrange(
                        "a p b c -> p (a b) c" if name in ("wqn", "wog") else "a p b c d -> p (a b) c d" if name == "wqr" else "a p b -> p (a b)"))
                    sp.dma_start(wqn[:], pick("wqn")).then_inc(a1["w_in"], 16)
                    sp.dma_start(wkT[:], pick("wkT")).then_inc(a1["w_in"], 16)
                    for h in range(4):
                        src = A["wqr"][g, :, h] if isinstance(g, int) else A["wqr"][bass.ds(g, 1), :, h].rearrange("a p b c -> p (a b) c")
                        sp.dma_start(WQ[:, h, :, 64:128], src).then_inc(a1["w_in"], 16)
                    sp.dma_start(WK[:, 64:128], pick("wkr")).then_inc(a1["w_in"], 16)
                    sp.dma_start(wog[:], pick("wog")).then_inc(a1["w_in"], 16)
                    sp.dma_start(wvT[:], pick("wvT")).then_inc(a1["w_in"], 16)

                sp.dma_start(wc[:], A["wc"]).then_inc(a1["wt_in"], 16)
                sp.dma_start(rope[:], A["c_rope"]).then_inc(a1["wt_in"], 16)
                sp.dma_start(self_[:], A["c_sel"]).then_inc(a1["wt_in"], 16)
                sp.dma_start(WK[:, 0:64], A["c_ident"][0:64, 0:64]).then_inc(a1["wt_in"], 16)
                group_weights(0)

                def neg_rows(n, par):
                    sp.wait_ge(a1["neg"], n + 1)
                    for part in range(2):
                        sp.dma_start(MR[4 * part:4 * part + 4, par, :], mb1[:, part, :]).then_inc(a1[f"row{par}"], 16)

                sp.wait_ge(a1["made"], 3)
                neg_rows(0, 0)
                sp.wait_ge(a1["x_ready"], x1_index(0, "V", 0) + 1)
                group_weights(1)
                neg_rows(1, 1)
                with sp.Fori(0, 3) as k:
                    neg_rows(2 * k + 2, 0)
                    g = sp.snap(k + 2)
                    sp.wait_ge(a1["x_ready"], x1_index(2 * k + 2, "V", "even") + 1)
                    group_weights(g)
                    neg_rows(2 * k + 3, 1)
                sp.wait_ge(a1["w_in"], 16 * 9 * 5)

            experts(moe[0], 0)
            sp.wait_ge(moe[0]["added"], 2 * NT)
            attention1()
            sp.wait_ge(a1["x_used"], x1_index(8, "O3", "end") + 1)
            experts(moe[1], 1)
            sp.wait_ge(moe[1]["added"], 2 * NT)
            sp.dma_start(A["out"].rearrange("(t p) d -> p t d", p=P), X[:]).then_inc(out_done, 16)
            sp.wait_ge(out_done, 16)
            sp.wait_ge(zero_in, 16)

        @block.gpsimd
        def _(pool):
            nc.gpsimd.memset(VS[:], 0.0).then_inc(pool_ready, 1)
            pool.wait_ge(pool_ready, 1)
            nc.gpsimd.memset(VS[:, :, :, :, 16:17].rearrange("p a b h o -> p (a b h) o"), 1.0).then_inc(pool_ready, 1)
            pool.wait_ge(w_in, 64)
            pool.wait_ge(LN[0]["xn"], NT)
            nc.gpsimd.tensor_tensor(X[:], X[:], bob[:, None, :].to_broadcast([P, NT, D]), ALU.add).then_inc(bo_added, 1)
            pool.wait_ge(v_taken, NT // 2)
            pool.wait_ge(pool_ready, 2)

            def stage(n, g, b):
                for kt in range(TB):
                    src = V[:, b * TB + kt, bass.ds(g * 64, 64)] if not isinstance(g, int) else V[:, b * TB + kt, g * 64:g * 64 + 64]
                    last = nc.gpsimd.tensor_copy(VS[:, b, kt, :, 0:16], src.rearrange("p (h d) -> p h d", h=4))
                last.then_inc(a0["staged"], 1)

            stage(0, 0, 0)
            stage(1, 0, 1)
            with pool.Fori(0, 3) as k:
                g = pool.snap(k + 1)
                pool.wait_ge(a0["pv"], 24 * (2 * k + 1))
                pool.wait_ge(pool_ready, 2)
                stage(2 * k + 2, g, 0)
                pool.wait_ge(a0["pv"], 24 * (2 * k + 2))
                pool.wait_ge(pool_ready, 2)
                stage(2 * k + 3, g, 1)

            def route(m):
                pool.wait_ge(zero_in, 16)
                pool.wait_ge(m["slot"], 2)
                for i in range(NT):
                    for j in range(2):
                        nc.gpsimd.indirect_dma_start(slots, bass.IndirectOffsetOnAxis(slot[:, j, i:i + 1], 0), XN[:, i, :], None).then_inc(m["scattered"], 16)
                for j in range(2):
                    pool.wait_ge(m[f"stored{j}"], 16 * NTILE // 2)
                for i in range(NT):
                    if i >= 4:
                        pool.wait_ge(m["added"], 2 * (i - 3))
                    for j in range(2):
                        nc.gpsimd.indirect_dma_start(yg[:, i % 4, j, :], None, outs, bass.IndirectOffsetOnAxis(slot[:, j, i:i + 1], 0)).then_inc(m[f"got{i % 4}"], 16)

            def attention1():
                pool.wait_ge(moe[0]["added"], 2 * NT)
                nc.gpsimd.memset(r2[:], 0.0).then_inc(a1["made"], 1)
                nc.gpsimd.memset(MR[:], 0.0).then_inc(a1["made"], 1)
                nc.gpsimd.memset(CA[:, :, 64:65], 1.0).then_inc(a1["made"], 1)

                def chunk(c, par, use):
                    b = CHUNKS.index(use) % 2
                    lo = int(use[-1]) * QC
                    low = KL[:, par, lo:lo + QC] if use[0] == "K" else QL[:, par, int(use[1]), lo:lo + QC]
                    high = KH[:, par, lo:lo + QC] if use[0] == "K" else QH[:, par, int(use[1]), lo:lo + QC]
                    pool.wait_ge(a1["plain"], c + 1)
                    pool.wait_ge(a1["roped"], c + 1)
                    nc.gpsimd.tensor_tensor(F[:, b, :], r1[:, b, :], r2[:, b, :], ALU.add).then_inc(a1["summed"], 1)
                    pool.wait_ge(a1["hi_ready"], c + 1)
                    nc.gpsimd.tensor_tensor(low, F[:, b, :], high.bitcast(F32), ALU.subtract).then_inc(a1["split"], 1)

                def front(n, par):
                    for i, use in enumerate(CHUNKS):
                        chunk(10 * n + i, par, use)

                front(0, 0)
                front(1, 1)
                with pool.Fori(0, 3) as k:
                    front(2 * k + 2, 0)
                    front(2 * k + 3, 1)

            route(moe[0])
            attention1()
            route(moe[1])

        @block.scalar
        def _(act):
            def layer_norm(ln):
                act.wait_ge(ln["var"], 1)
                nc.scalar.activation(rs[:, 1, :], rs[:, 0, :], ACT.Sqrt).then_inc(ln["sd"], 1)
                for i in range(NT // 2):
                    act.wait_ge(ln["t"], i + 1)
                    nc.scalar.activation(XT[:, :, 2 * i * P:(2 * i + 2) * P], PS[:, i % 4, :].rearrange("p (c t) -> p c t", c=KC),
                                         ACT.Copy).then_inc(ln["xt"], 1)

            layer_norm(LN[0])

            def probs(n, s, wait_free):
                qc, kt, pair = SLOTS[s]
                lo = first_query(qc, kt)
                act.wait_ge(a0["scores"], 24 * n + s + 1)
                if wait_free:
                    act.wait_ge(a0["pv"], 24 * n + s - 2)
                nc.scalar.activation(PT[:, s % 3, :, lo:QC], PS[:, 2 * (s % 2):2 * (s % 2) + 2, lo:QC], ACT.Exp,
                                     scale=0.25).then_inc(a0["probs"], 1)

            def high_part(n, i, par, kind, at):
                side, c = i // 2, i % 2
                act.wait_ge(a0["x_used"], x_index(at, f"P{i}", kind) + 1)
                bias = cg[:, par, 2 * side:2 * side + 1]
                nc.scalar.activation(QKs[:, 2 * side, c * QC:(c + 1) * QC], tq[:, i % 2, :], ACT.Identity, bias=bias).then_inc(a0["hi_ready"], 1)

            def evac(n, qc, kind):
                act.wait_ge(a0["pv"], 24 * n + (8 if qc == 0 else 24))
                if not (kind == 0 and qc == 0):
                    if qc == 0:
                        act.wait_ge(a0["x_used"], x_index(n, "B1", kind) + 1)
                    else:
                        act.wait_ge(a0["x_used"], x_index(n, "B0", kind) + 1)
                nc.scalar.activation(oT[:], psO, ACT.Copy).then_inc(a0["evac"], 1)

            def step(n, b, kind):
                for s in range(24):
                    probs(n, s, not (isinstance(n, int) and n == 0 and s < 3))
                    if kind != 7 and s < 4:
                        high_part(n + 1, s, 1 - b, kind, n)
                    if s == 10:
                        evac(n, 0, kind)
                evac(n, 1, kind)

            for i in range(4):
                high_part(0, i, 0, "front", 0)
            step(0, 0, 0)
            with act.Fori(0, 3) as k:
                step(2 * k + 1, 1, 1)
                step(2 * k + 2, 0, 1)
            step(7, 1, 7)

            def experts(m, ln):
                layer_norm(ln)
                act.wait_ge(m["shifted"], 1)
                nc.scalar.activation(R[:, 1], R[:, 0], ACT.Exp).then_inc(m["exps"], 1)

                def silu(q, b, c):
                    act.wait_ge(m["u"], q + 1)
                    if c:
                        act.wait_ge(m["h"], q - 1)
                    nc.scalar.activation(sg[:, b, :], PS[:, b, 0:HID], ACT.Silu).then_inc(m["sg"], 1)

                def turned_x(g, b, c):
                    act.wait_ge(m["t"], g + 1)
                    if c:
                        act.wait_ge(m["u"], NSH + g - 1)
                    nc.scalar.activation(xTs[:, b], PS[:, 2 + b, 0:D].rearrange("p (c t) -> p c t", c=KC), ACT.Copy).then_inc(m["xT"], 1)

                def turned_h(q, b, c):
                    act.wait_ge(m["ht"], q + 1)
                    if c:
                        act.wait_ge(m["d"], q - 1)
                    nc.scalar.activation(hT[:, b], PS[0:HH, 4 + b, 0:2 * P].rearrange("p (c t) -> p c t", c=2), ACT.Copy).then_inc(m["hT"], 1)

                def step(q, g, b, c):
                    silu(q, b, c or q >= 2)
                    if g is not None:
                        turned_x(g, 1 - b, c or g >= 2)
                    if c or q >= 1:
                        turned_h(q - 1, 1 - b, c or q >= 3)

                for q in range(NSH):
                    step(q, 0 if q == NSH - 1 else None, q % 2, False)
                step(NSH, 1, 0, False)
                step(NSH + 1, 2, 1, False)
                with act.Fori(0, NTILE // 2 - 2) as k:
                    step(NSH + 2 + 2 * k, 2 * k + 3, 0, True)
                    step(NSH + 3 + 2 * k, 2 * k + 4, 1, True)
                q = NSH + NTILE - 2
                step(q, NTILE - 1, 0, False)
                step(q + 1, None, 1, False)
                turned_h(q + 1, 1, True)

            experts(moe[0], LN[1])

            def attention1():
                layer_norm(LN[2])
                for i in range(4):
                    act.wait_ge(a1["c_ready"], i + 1)
                    nc.scalar.activation(cT[:, i * QC:(i + 1) * QC], PS[0:64, 4 + i % 2, :], ACT.Copy).then_inc(a1["cT"], 1)
                act.wait_ge(a1["made"], 3)
                for i in range(2):
                    act.wait_ge(a1["ct_turned"], i + 1)
                    nc.scalar.activation(CA[:, 8 * i:8 * i + 8, 0:64], PS[:, 6 + i, :].rearrange("p (t c) -> p t c", c=64), ACT.Copy).then_inc(a1["CA"], 1)

                def plain(n, use, kind, at):
                    i = CHUNKS.index(use)
                    c = 10 * n + i
                    act.wait_ge(a1["x_ready"], x1_index(at, use, kind) + 1)
                    if not (isinstance(c, int) and c < 2):
                        act.wait_ge(a1["summed"], c - 1)
                    nc.scalar.activation(r1[0:64, i % 2, :], psX[0:64, :], ACT.Copy).then_inc(a1["plain"], 1)

                def high_part(n, use, par):
                    i = CHUNKS.index(use)
                    c = 10 * n + i
                    lo = int(use[-1]) * QC
                    high = KH[:, par, lo:lo + QC] if use[0] == "K" else QH[:, par, int(use[1]), lo:lo + QC]
                    act.wait_ge(a1["summed"], c + 1)
                    nc.scalar.activation(high, F[:, i % 2, :], ACT.Copy).then_inc(a1["hi_ready"], 1)

                def probs(n, s):
                    h, qc, kt = SLOTS1[s]
                    lo = first_query(qc, kt)
                    act.wait_ge(a1["scores"], 48 * n + s + 1)
                    if not (isinstance(n, int) and n == 0 and s < 4):
                        act.wait_ge(a1["pv"], 48 * n + s - 3)
                    nc.scalar.activation(PT1[:, s % 4, lo:QC], PS[:, s % 3, lo:QC], ACT.Exp, scale=SCALE1).then_inc(a1["probs"], 1)

                def turned(n, use, kind):
                    pair, qc = int(use[1]) // 2, int(use[1]) % 2
                    act.wait_ge(a1["x_ready"], x1_index(n, use, kind) + 1)
                    nc.scalar.activation(oN1[:, pair, qc * QC:(qc + 1) * QC], psX, ACT.Copy).then_inc(a1["x_used"], 1)

                def step(n, b, kind):
                    for s in range(48):
                        probs(n, s)
                        for use in X1_AT[s]:
                            if use[0] == "N" and has1(use, kind):
                                turned(n, use, kind)
                        if kind != 7:
                            for use in HI_AT.get(s, ()):
                                high_part(n + 1, use, 1 - b)
                            for use in X1_AT[s]:
                                if use in CHUNKS:
                                    plain(n + 1, use, kind, n)

                for use in CHUNKS:
                    plain(0, use, "front", 0)
                    high_part(0, use, 0)
                step(0, 0, 0)
                with act.Fori(0, 3) as k:
                    step(2 * k + 1, 1, "odd")
                    step(2 * k + 2, 0, "even")
                step(7, 1, 7)
                turned(8, "N3", "end")

            attention1()
            experts(moe[1], LN[3])

        @block.vector
        def _(dve):
            def link(ins):
                dve.wait_ge(dve_done, dv.up(ins))

            dve.wait_ge(const_in, 128)
            nc.vector.tensor_copy(identb[:], ident[:]).then_inc(consts_made, 1)
            nc.vector.tensor_copy(masks[:], masksf[:]).then_inc(consts_made, 1)
            nc.vector.tensor_tensor(coef[:, :, 0], coef[:, :, 0], bqk[:, :, 0], ALU.add).then_inc(coef_ready, 1)
            nc.vector.tensor_tensor(coef[:, :, 2], coef[:, :, 2], bqk[:, :, 1], ALU.add).then_inc(coef_ready, 1)
            dve.wait_ge(coef_ready, 2)

            link(nc.vector.memset(MX[:], 0.0))
            nc.vector.memset(ones[:], 1.0)
            nc.vector.memset(zeros[:], 0.0).then_inc(zero_made, 1)

            def layer_norm(ln):
                for i in range(NT):
                    last = nc.vector.bn_stats(stats[:, i, :], X[:, i, :])
                link(last)
                for i in range(NT):
                    last = nc.vector.bn_aggr(mv[:, i, :], stats[:, i, :])
                link(last)
                nc.vector.tensor_scalar(rs[:, 0, :], mv[:, :, 1], EPS, None, ALU.add).then_inc(ln["var"], 1)
                dve.wait_ge(ln["var"], 1)
                dve.wait_ge(ln["sd"], 1)
                link(nc.vector.reciprocal(rs[:, 2, :], rs[:, 1, :]))
                link(nc.vector.tensor_tensor(rs[:, 3, :], rs[:, 2, :], rs[:, 2, :], ALU.mult))
                link(nc.vector.tensor_tensor(rs[:, 3, :], rs[:, 3, :], rs[:, 0, :], ALU.mult))
                link(nc.vector.tensor_scalar(rs[:, 3, :], rs[:, 3, :], -0.5, 1.5, ALU.mult, ALU.add))
                link(nc.vector.tensor_tensor(rs[:, 1, :], rs[:, 2, :], rs[:, 3, :], ALU.mult))
                for i in range(NT):
                    nc.vector.tensor_scalar(XN[:, i, :], X[:, i, :], mv[:, i, 0:1], rs[:, 1, i:i + 1], ALU.subtract, ALU.mult).then_inc(ln["xn"], 1)

            dve.wait_ge(x_in, 64)
            layer_norm(LN[0])
            for i in range(NT // 2):
                dve.wait_ge(v_ready, i + 1)
                if i == 0:
                    dve.wait_ge(w_in, 64)
                nc.vector.tensor_tensor(V[:, 2 * i:2 * i + 2, :], PS[:, 4 + i % 2, :].rearrange("p (t n) -> p t n", t=2),
                                        bvb[:, None, :].to_broadcast([P, 2, D]), ALU.add).then_inc(v_taken, 1)

            def pick(n, par, g):
                src = coef[:, g, :] if isinstance(g, int) else coef[:, bass.ds(g, 1), :].rearrange("p a b -> p (a b)")
                nc.vector.tensor_copy(cg[:, par, :], src).then_inc(a0["cg"], 1)
                dve.wait_ge(a0["cg"], n + 1)

            def with_positions(n, i, par, kind, at):
                side, c = i // 2, i % 2
                dve.wait_ge(a0["x_ready"], x_index(at, f"P{i}", kind) + 1)
                col = cg[:, par, 2 * side + 1:2 * side + 2]
                if i >= 2:
                    dve.wait_ge(a0["split"], 4 * n + i - 1)
                nc.vector.scalar_tensor_tensor(tq[:, i % 2, :], pos[:, c * QC:(c + 1) * QC], col, psX, ALU.mult, ALU.add).then_inc(a0["x_used"], 1)

            def low_part(n, i, par):
                side, c = i // 2, i % 2
                col = cg[:, par, 2 * side:2 * side + 1]
                dve.wait_ge(a0["hi_ready"], 4 * n + i + 1)
                nc.vector.scalar_tensor_tensor(QKs[:, 2 * side + 1, c * QC:(c + 1) * QC], tq[:, i % 2, :], col,
                                               QKs[:, 2 * side, c * QC:(c + 1) * QC].bitcast(F32), ALU.add, ALU.subtract).then_inc(a0["split"], 1)

            def row_max(n, par, i):
                group = GROUPS[i]
                dve.wait_ge(a0["max_scored"], 24 * n + i + 1)
                if len(group) == 2:
                    (h, qt, _), _ = group
                    w = (qt + 2) * P
                    src = psM.rearrange("p (a b) -> p a b", a=2)[:, :, 0:w]
                    nc.vector.reduce_max(MX[:, par, 8 * h + qt:8 * h + qt + 2], src, AXX).then_inc(a0["max_taken"], 1)
                else:
                    (h, qt, _), = group
                    nc.vector.reduce_max(MX[:, par, 8 * h + qt:8 * h + qt + 1], psM[:, 0:(qt + 1) * P], AXX).then_inc(a0["max_taken"], 1)

            def negate(n, kind, at):
                dve.wait_ge(a0["x_ready"], x_index(at, "T", kind) + 1)
                nc.vector.tensor_scalar(mneg[:], psX[0:32, 0:P], -1.0, None, ALU.mult).then_inc(a0["x_used"], 1)
                dve.wait_ge(a0["x_used"], x_index(at, "T", kind) + 1)
                if not (isinstance(n, int) and n == 0):
                    pass
                nc.vector.tensor_copy(mh[:, 0, :], mneg[:]).then_inc(a0["neg_hi"], 1)
                dve.wait_ge(a0["neg_hi"], n + 1)
                nc.vector.tensor_tensor(mh[:, 1, :], mneg[:], mh[:, 0, :].bitcast(F32), ALU.subtract).then_inc(a0["neg"], 1)

            def reciprocals(n, kind, use):
                dve.wait_ge(a0["x_ready"], x_index(n, use, kind) + 1)
                nc.vector.reciprocal(rc[:], psX[:, 0:16]).then_inc(a0["x_used"], 1)
                dve.wait_ge(a0["x_used"], x_index(n, use, kind) + 1)
                nc.vector.tensor_copy(rb[:], rc[:, :, None].to_broadcast([P, 16, 32])).then_inc(a0["recip"], 1)

            def normalise(n, kind, use):
                dve.wait_ge(a0["x_ready"], x_index(n, use, kind) + 1)
                nc.vector.tensor_tensor(oN[:], oT[:], psX, ALU.mult).then_inc(a0["x_used"], 1)

            def add_out(n, kind, use, b, qc):
                half = use[-1] == "b"
                t0 = b * TB + qc * 4 + 2 * half
                dve.wait_ge(a0["x_ready"], x_index(n, use, kind) + 1)
                nc.vector.tensor_tensor(X[:, t0:t0 + 2, :], X[:, t0:t0 + 2, :], psX.rearrange("p (t n) -> p t n", t=2), ALU.add).then_inc(a0["x_used"], 1)

            def step(n, b, g1, kind):
                if kind != 7:
                    pick(n + 1, 1 - b, g1)
                for s in range(24):
                    use = X_AT.get(s)
                    if use in ORDERS[kind]:
                        if use[0] == "P":
                            with_positions(n + 1, int(use[1]), 1 - b, kind, n)
                            if s > 0:
                                low_part(n + 1, s - 1, 1 - b)
                        elif use[0] == "S":
                            reciprocals(n, kind, use)
                        elif use[0] == "B":
                            normalise(n, kind, use)
                        else:
                            qc = int(use[1])
                            add_out(n, kind, use, (1 - b) if qc == 1 else b, qc)
                    if kind != 7:
                        if s == 4:
                            low_part(n + 1, 3, 1 - b)
                        for i in MAX_AT[s]:
                            row_max(n + 1, 1 - b, i)
                if kind != 7:
                    negate(n + 1, kind, n)

            dve.wait_ge(bo_added, 1)
            pick(0, 0, 0)
            for i in range(4):
                with_positions(0, i, 0, "front", 0)
                low_part(0, i, 0)
            for i in range(len(GROUPS)):
                row_max(0, 0, i)
            negate(0, "front", 0)
            step(0, 0, 0, 0)
            with dve.Fori(0, 3) as k:
                g = dve.snap(k + 1)
                step(2 * k + 1, 1, g, 1)
                step(2 * k + 2, 0, g, 1)
            step(7, 1, 0, 7)
            for use in PREV:
                if use == "S1":
                    reciprocals(8, "end", use)
                elif use == "B1":
                    normalise(8, "end", use)
                else:
                    add_out(8, "end", use, 1, 1)

            def experts(m, n):
                def bc(a):
                    return a[:, :, None].to_broadcast([P, NT, 16])

                rev = small[:, None, 0:16].to_broadcast([P, NT, 16])
                tt, ts = nc.vector.tensor_tensor, nc.vector.tensor_scalar
                def hidden(q, b):
                    dve.wait_ge(m["sg"], q + 1)
                    if not isinstance(q, int) or q >= 2:
                        dve.wait_ge(m["ht"], q - 1)
                    tt(hb[:, b, :], sg[:, b, :], PS[:, b, HID:2 * HID], ALU.mult).then_inc(m["h"], 1)

                def shared_out(q):
                    i = q // 2
                    dve.wait_ge(m["d"], q + 1)
                    if q % 2:
                        dve.wait_ge(m["y"], q)
                    tt(X[:, i, :], X[:, i, :], PS[:, 6 + q % 2, 0:D], ALU.add).then_inc(m["y"], 1)

                def shared(q):
                    hidden(q, q % 2)
                    if q >= 2:
                        shared_out(q - 2)

                logits = PS[:, 2, 0:256].rearrange("p (t e) -> p t e", e=16)
                dve.wait_ge(m["logits"], 1)
                link(nc.vector.reduce_max(rt[:, 0], logits, AXX))
                tt(R[:, 0], logits, bc(rt[:, 0]), ALU.subtract).then_inc(m["shifted"], 1)
                dve.wait_ge(m["exps"], 1)
                link(nc.vector.reduce_sum(rt[:, 1], R[:, 1], AXX))
                link(nc.vector.reciprocal(rt[:, 1], rt[:, 1]))
                link(tt(R[:, 2], R[:, 1], bc(rt[:, 1]), ALU.mult))
                shared(0)
                src = R[:, 2]
                for j in range(2):
                    link(nc.vector.reduce_max(rt[:, 2 + j], src, AXX))
                    link(tt(R[:, 3], src, bc(rt[:, 2 + j]), ALU.is_equal))
                    link(tt(R[:, 3], R[:, 3], rev, ALU.mult))
                    shared(2 * j + 1)
                    link(nc.vector.reduce_max(rt[:, 4 + j], R[:, 3], AXX))
                    link(tt(R[:, 4 + j], rev, bc(rt[:, 4 + j]), ALU.is_equal))
                    if j == 0:
                        link(nc.vector.scalar_tensor_tensor(R[:, 6], R[:, 4], -2.0, R[:, 2], ALU.mult, ALU.add))
                        src = R[:, 6]
                        shared(2)
                tt(R[:, 7], R[:, 4], R[:, 5], ALU.add).then_inc(m["onehot"], 1)
                shared(4)
                shared(COUNT_AT)
                nc.vector.memset(carry[:, 0, :], 0.0)
                dve.wait_ge(m["counted"], 1)
                totals = PS[:, 3, 256:512].rearrange("p (t e) -> p t e", e=16)
                ranks = PS[:, 3, 0:256].rearrange("p (t e) -> p t e", e=16)
                link(nc.vector.tensor_copy(carry[:, 1, :], totals[:, 0, :]))
                for i in range(1, NT):
                    link(tt(carry[:, i + 1, :], carry[:, i, :], totals[:, i, :], ALU.add))
                    if i % 7 == 0:
                        shared(COUNT_AT + i // 7)
                link(ts(tl[:, 0], carry[:, NT, :], 1.0 / P, 127.0 / 128 - 127.0 / 256, ALU.mult, ALU.add))
                link(nc.vector.tensor_copy(tli[:], tl[:, 0]))
                link(nc.vector.tensor_copy(tl[:, 0], tli[:]))
                shared(COUNT_AT + 3)
                link(tt(lt[:], small[:, 16:272].rearrange("p (a b) -> p a b", b=16), tl[:, 0, None, :].to_broadcast([P, 16, 16]), ALU.mult))
                link(nc.vector.reduce_sum(tl[:, 1], lt[:], AXX))
                link(tt(tl[:, 2], tl[:, 1], tl[:, 0], ALU.add))
                link(ts(tl[:, 3], tl[:, 1], float(P), None, ALU.mult))
                shared(COUNT_AT + 4)
                link(tt(R[:, 3], carry[:, 0:NT, :], ranks, ALU.add))
                link(tt(R[:, 3], R[:, 3], tl[:, 3, None, :].to_broadcast([P, NT, 16]), ALU.add))
                for j in range(2):
                    link(tt(R[:, 6], R[:, 3], R[:, 4 + j], ALU.mult))
                    link(nc.vector.reduce_sum(rt[:, 6 + j], R[:, 6], AXX))
                    nc.vector.tensor_copy(slot[:, j, :], rt[:, 6 + j]).then_inc(m["slot"], 1)
                    shared(COUNT_AT + 5 + j)
                link(tt(owner[:], tl[:, 2, None, :].to_broadcast([P, NTILE, 16]), small[:, 272:].rearrange("p (g e) -> p g e", e=16), ALU.is_le))
                link(nc.vector.reduce_sum(eidf[:], owner[:], AXX))
                shared(COUNT_AT + 7)
                link(ts(eidf[:], eidf[:], 15.0, None, ALU.min))
                nc.vector.tensor_copy(eid[:], eidf[:]).then_inc(m["eid"], 1)

                def tile_out(q, b):
                    dve.wait_ge(m["d"], q + 1)
                    if not isinstance(q, int) or q >= NSH + 2:
                        dve.wait_ge(m[f"stored{b}"], 16 * ((q - NSH) // 2) if isinstance(q, int) else stored)
                    nc.vector.tensor_copy(ys[:, b, :], PS[:, 6 + b, 0:D]).then_inc(m["y"], 1)

                for q in range(COUNT_AT + 8, NSH):
                    shared(q)
                for q in range(NSH, NSH + 4):
                    hidden(q, q % 2)
                    if q < NSH + 2:
                        shared_out(q - 2)
                    else:
                        tile_out(q - 2, q % 2)
                with dve.Fori(0, NTILE // 2 - 2) as k:
                    for j in range(2):
                        q = NSH + 4 + 2 * k + j
                        hidden(q, j)
                        stored = 16 * k + 16
                        tile_out(q - 2, j)
                for q in range(NSH + NTILE - 2, NSH + NTILE):
                    tile_out(q, q % 2)
                for i in range(NT):
                    dve.wait_ge(m[f"got{i % 4}"], 32 * (i // 4 + 1))
                    for j in range(2):
                        if j:
                            dve.wait_ge(m["added"], 2 * i + 1)
                        nc.vector.scalar_tensor_tensor(X[:, i, :], yg[:, i % 4, j, :], rt[:, 2 + j, i:i + 1], X[:, i, :], ALU.mult, ALU.add).then_inc(m["added"], 1)

            dve.wait_ge(a0["x_used"], x_index(8, "W1b", "end") + 1)
            layer_norm(LN[1])
            experts(moe[0], 0)

            def attention1():
                dve.wait_ge(a1["wt_in"], 64)
                nc.vector.tensor_copy(selb[:], self_[:]).then_inc(a1["sel"], 1)
                link(nc.vector.memset(MX1[:], 0.0))

                def rotate(n, use, kind, at):
                    i = CHUNKS.index(use)
                    c, j = 10 * n + i, i % 2
                    cols = slice(int(use[-1]) * QC, int(use[-1]) * QC + QC)
                    dve.wait_ge(a1["x_ready"], x1_index(at, use, kind) + 1)
                    if not (isinstance(c, int) and c < 2):
                        dve.wait_ge(a1["summed"], c - 1)
                    nc.vector.tensor_tensor(r2[64:96, j, :], psX[96:128, :], rope[96:128, 1, cols], ALU.mult)
                    nc.vector.tensor_tensor(r2[96:128, j, :], psX[64:96, :], rope[64:96, 1, cols], ALU.mult)
                    nc.vector.tensor_tensor(r1[64:128, j, :], psX[64:128, :], rope[64:128, 0, cols], ALU.mult).then_inc(a1["roped"], 1)
                    dve.wait_ge(a1["plain"], c + 1)
                    dve.wait_ge(a1["roped"], c + 1)
                    nc.vector.tensor_copy(rt1[:], ones[:, 0:1]).then_inc(a1["x_used"], 1)

                def row_max(n, par, i):
                    group = GROUPS[i]
                    h, qt, _ = group[0]
                    dve.wait_ge(a1["max_scored"], 24 * n + i + 1)
                    if len(group) == 2:
                        src = psM.rearrange("p (a b) -> p a b", a=2)[:, :, 0:(qt + 2) * P]
                        nc.vector.reduce_max(MX1[:, par, 8 * h + qt:8 * h + qt + 2], src, AXX).then_inc(a1["max_taken"], 1)
                    else:
                        nc.vector.reduce_max(MX1[:, par, 8 * h + qt:8 * h + qt + 1], psM[:, 0:(qt + 1) * P], AXX).then_inc(a1["max_taken"], 1)

                def negate(n, kind, at):
                    i = x1_index(at, "T", kind)
                    dve.wait_ge(a1["x_ready"], i + 1)
                    nc.vector.tensor_scalar(mn1[:, 0, :], psX[0:32, 0:P], -1.0, None, ALU.mult).then_inc(a1["x_used"], 1)
                    dve.wait_ge(a1["x_used"], i + 1)
                    nc.vector.tensor_copy(mb1[:, 0, :], mn1[:, 0, :]).then_inc(a1["neg_mid"], 1)
                    dve.wait_ge(a1["neg_mid"], 2 * n + 1)
                    nc.vector.tensor_tensor(mn1[:, 1, :], mn1[:, 0, :], mb1[:, 0, :], ALU.subtract).then_inc(a1["neg_mid"], 1)
                    dve.wait_ge(a1["neg_mid"], 2 * n + 2)
                    nc.vector.tensor_copy(mb1[:, 1, :], mn1[:, 1, :]).then_inc(a1["neg"], 1)

                def other(n, use, kind, b):
                    i = x1_index(n, use, kind)
                    dve.wait_ge(a1["x_ready"], i + 1)
                    if use == "A":
                        nc.vector.tensor_copy(WQ[:, :, :, 0:64].rearrange("p h k c -> p (h k) c"), psX.rearrange("p (a c) -> p a c", c=64)).then_inc(a1["x_used"], 1)
                    elif use == "V":
                        nc.vector.tensor_copy(WVO[:].rearrange("p a n -> p (a n)"), psX).then_inc(a1["x_used"], 1)
                    else:
                        t0 = (1 - b) * TB + 2 * int(use[1])
                        nc.vector.tensor_tensor(X[:, t0:t0 + 2, :], X[:, t0:t0 + 2, :], psX.rearrange("p (t n) -> p t n", t=2), ALU.add).then_inc(a1["x_used"], 1)

                def finish(n, c):
                    h, qc, i = c // 2, c % 2, 8 * n + c
                    out = PS[:, 3 if qc == 0 else 6, 0:260].rearrange("p (t e) -> p t e", e=65)
                    dve.wait_ge(a1["pv"], 48 * n + 12 * h + (4 if qc == 0 else 12))
                    if not (isinstance(n, int) and n == 0 and c < 2):
                        dve.wait_ge(a1["evac"], i - 1)
                    nc.vector.reciprocal(rc1[:, qc, :], out[:, :, 64]).then_inc(a1["recip"], 1)
                    dve.wait_ge(a1["recip"], i + 1)
                    nc.vector.tensor_tensor(oq1[:, h // 2, 4 * qc:4 * qc + 4, h % 2, :], out[:, :, 0:64],
                                            rc1[:, qc, :, None].to_broadcast([P, 4, 64]), ALU.mult).then_inc(a1["evac"], 1)

                def step(n, b, kind):
                    for s in range(48):
                        if s == 2 and kind != 0:
                            finish(n - 1, 7)
                        for h in range(4):
                            if s == 12 * h + 6:
                                finish(n, 2 * h)
                            if s == 12 * h + 14:
                                finish(n, 2 * h + 1)
                        for use in X1_AT[s]:
                            if has1(use, kind) and use[0] != "N":
                                if use in CHUNKS:
                                    rotate(n + 1, use, kind, n)
                                else:
                                    other(n, use, kind, b)
                        if kind != 7:
                            for i in MAX1_AT[s]:
                                row_max(n + 1, 1 - b, i)
                    if kind != 7:
                        negate(n + 1, kind, n)

                other(0, "A", "front", 0)
                for use in CHUNKS:
                    rotate(0, use, "front", 0)
                for i in range(len(GROUPS)):
                    row_max(0, 0, i)
                negate(0, "front", 0)
                step(0, 0, 0)
                with dve.Fori(0, 3) as k:
                    step(2 * k + 1, 1, "odd")
                    step(2 * k + 2, 0, "even")
                step(7, 1, 7)
                finish(7, 7)
                for use in PREV1[1:]:
                    other(8, use, "end", 0)

            dve.wait_ge(moe[0]["added"], 2 * NT)
            layer_norm(LN[2])
            attention1()
            dve.wait_ge(a1["x_used"], x1_index(8, "O3", "end") + 1)
            layer_norm(LN[3])
            experts(moe[1], 1)

        @block.tensor
        def _(pe):
            pe.wait_ge(consts_made, 2)

            def layer_norm(ln):
                for i in range(NT // 2):
                    pe.wait_ge(ln["xn"], 2 * i + 2)
                    if i >= 4:
                        pe.wait_ge(ln["xt"], i - 3)
                    for c in range(KC):
                        for t in range(2):
                            last = nc.tensor.transpose(PS[:, i % 4, (2 * c + t) * P:(2 * c + t + 1) * P], XN[:, 2 * i + t, c * P:(c + 1) * P], ident[:])
                    last.then_inc(ln["t"], 1)

            layer_norm(LN[0])
            pe.wait_ge(w_in, 64)
            for i in range(NT // 2):
                pe.wait_ge(LN[0]["xt"], i + 1)
                if i >= 2:
                    pe.wait_ge(v_taken, i - 1)
                for t in range(2):
                    for c in range(KC):
                        last = nc.tensor.matmul(PS[:, 4 + i % 2, t * D:(t + 1) * D], XT[:, c, (2 * i + t) * P:(2 * i + t + 1) * P], wv[:, c, :],
                                                start=(c == 0), stop=(c == KC - 1))
                last.then_inc(v_ready, 1)

            def free_x(n, use, kind):
                i = x_index(n, use, kind)
                if not (isinstance(i, int) and i == 0):
                    pe.wait_ge(a0["x_used"], i)

            def max_scores(n, par, i, k_round):
                if i % 6 == 0:
                    pe.wait_ge(copied[par][i // 6], k_round)
                if not (isinstance(n, int) and n == 0 and i == 0):
                    pe.wait_ge(a0["max_taken"], 24 * n + i)
                for h, qt, at in GROUPS[i]:
                    w = (qt + 1) * P
                    q = QS[:, par, h, qt * P:(qt + 1) * P]
                    for k0 in range(0, w, QC):
                        k1 = min(w, k0 + QC)
                        diag = k1 == w
                        last = nc.tensor.matmul(psM[:, at + k0:at + k1], q, KS[:, par, h, k0:k1], start=True, stop=not diag)
                        if diag:
                            last = nc.tensor.matmul(psM[:, at + k1 - P:at + k1], identb[:], masks[:, 0, :], start=False, stop=True)
                    if len(GROUPS[i]) == 2 and at == 0:
                        last = nc.tensor.matmul(psM[:, at + w:at + w + P], identb[:], masks[:, 2, :], start=True, stop=True)
                last.then_inc(a0["max_scored"], 1)

            def turn(n, par, at, kind):
                free_x(at, "T", kind)
                pe.wait_ge(a0["max_taken"], 24 * n + 24)
                nc.tensor.transpose(psX[:, 0:P], MX[:, par, :], ident[:]).then_inc(a0["x_ready"], 1)

            def scores(n, par, s, first):
                qc, kt, pair = SLOTS[s]
                lo = first_query(qc, kt)
                diag = kt * P >= qc * QC
                if not (isinstance(n, int) and n == 0 and s < 2):
                    pe.wait_ge(a0["probs"], 24 * n + s - 1)
                for j in range(2):
                    h, bank = 2 * pair + j, 2 * (s % 2) + j
                    last = nc.tensor.matmul(PS[:, bank, lo:QC], KS[:, par, h, kt * P:(kt + 1) * P], QS[:, par, h, qc * QC + lo:(qc + 1) * QC],
                                            start=True, stop=not diag)
                    if diag:
                        last = nc.tensor.matmul(PS[:, bank, lo:lo + P], identb[:], masks[:, 1, :], start=False, stop=True)
                last.then_inc(a0["scores"], 1)

            def values(n, b, s):
                qc, kt, pair = SLOTS[s]
                lo = first_query(qc, kt)
                pe.wait_ge(a0["probs"], 24 * n + s + 1)
                if pair == 0 and kt == 0:
                    if not (isinstance(n, int) and n == 0 and qc == 0):
                        pe.wait_ge(a0["evac"], 2 * n + qc)
                    pe.wait_ge(a0["staged"], n + 1)
                for j in range(2):
                    h = 2 * pair + j
                    last = nc.tensor.matmul(psO[32 * h:32 * h + 32, lo:QC], VS[:, b, kt, h, :], PT[:, s % 3, j, lo:QC],
                                            start=(kt == 0), stop=(kt == (3 if qc == 0 else 7)), skip_group_check=True)
                last.then_inc(a0["pv"], 1)

            def sums(n, use, kind):
                free_x(n, use, kind)
                pe.wait_ge(a0["evac"], 2 * n + (1 if use[1] == "0" else 0))
                for t in range(4):
                    last = nc.tensor.matmul(psX[:, 4 * t:4 * t + 4], oT[:, t * P:(t + 1) * P], spread[:, 0:P:32], start=True, stop=True)
                last.then_inc(a0["x_ready"], 1)

            def spread_out(n, use, kind):
                pe.wait_ge(a0["recip"], 2 * n + (1 if use[1] == "0" else 0))
                for t in range(4):
                    last = nc.tensor.matmul(psX[:, t * P:(t + 1) * P], rb[:, 4 * t:4 * t + 4, :].rearrange("p a b -> p (a b)"), ident[:], start=True, stop=True)
                last.then_inc(a0["x_ready"], 1)

            def out_rows(n, use, kind, g):
                half, qc = use[-1] == "b", int(use[1])
                free_x(n, use, kind)
                for t in range(2):
                    w = wo0[:, g, :] if isinstance(g, int) else wo0[:, bass.ds(g, 1), :].rearrange("p a n -> p (a n)")
                    last = nc.tensor.matmul(psX[:, t * D:(t + 1) * D], oN[:, (2 * half + t) * P:(2 * half + t + 1) * P], w, start=True, stop=True)
                last.then_inc(a0["x_ready"], 1)

            def step(n, b, g, gprev, kind, k_here, k_next, w_need=None):
                pe.wait_ge(a0[f"row{b}"], k_here)
                for s in range(24):
                    scores(n, b, s, s == 0)
                    if s >= 2:
                        values(n, b, s - 2)
                    use = X_AT.get(s)
                    if use in ORDERS[kind]:
                        if use[0] == "P":
                            if use == "P0" and w_need is not None:
                                pe.wait_ge(a0["w_in"], w_need)
                            i = int(use[1])
                            side, c = i // 2, i % 2
                            free_x(n, use, kind)
                            for kc in range(KC):
                                last = nc.tensor.matmul(psX, wqk[:, 2 * side + kc, :], XT[:, kc, (1 - b) * SEQ + c * QC:(1 - b) * SEQ + (c + 1) * QC],
                                                        start=(kc == 0), stop=(kc == 1))
                            last.then_inc(a0["x_ready"], 1)
                        elif use[0] == "S":
                            sums(n, use, kind)
                        elif use[0] == "B":
                            spread_out(n, use, kind)
                        else:
                            out_rows(n, use, kind, gprev if use[1] == "1" else g)
                    if kind != 7:
                        for i in MAX_AT[s]:
                            max_scores(n + 1, 1 - b, i, k_next)
                values(n, b, 22)
                values(n, b, 23)
                if kind != 7:
                    turn(n + 1, 1 - b, n, kind)

            pe.wait_ge(v_taken, NT // 2)
            pe.wait_ge(LN[0]["xt"], NT // 2)
            pe.wait_ge(a0["w_in"], 16)
            for i in range(4):
                side, c = i // 2, i % 2
                free_x(0, f"P{i}", "front")
                for kc in range(KC):
                    last = nc.tensor.matmul(psX, wqk[:, 2 * side + kc, :], XT[:, kc, c * QC:(c + 1) * QC], start=(kc == 0), stop=(kc == 1))
                last.then_inc(a0["x_ready"], 1)
            for i in range(len(GROUPS)):
                max_scores(0, 0, i, 128)
            turn(0, 0, 0, "front")
            step(0, 0, 0, 0, 0, 32, 128)
            with pe.Fori(0, 3) as k:
                g1 = pe.snap(k + 1)
                step(2 * k + 1, 1, k, k, 1, 32 * k + 32, 128 * k + 256, 16 * k + 32)
                step(2 * k + 2, 0, g1, k, 1, 32 * k + 64, 128 * k + 256)
            step(7, 1, 3, 3, 7, 128, 0)
            for use in PREV:
                if use == "S1":
                    sums(8, use, "end")
                elif use == "B1":
                    spread_out(8, use, "end")
                else:
                    out_rows(8, use, "end", 3)

            def experts(m, ln):
                layer_norm(ln)
                pe.wait_ge(m["gate_in"], 16)
                pe.wait_ge(ln["xt"], NT // 2)
                for i in range(NT):
                    for kc in range(KC):
                        last = nc.tensor.matmul(PS[:, 2, i * 16:i * 16 + 16], XT[:, kc, i * P:(i + 1) * P], gw[:, kc, :], start=(kc == 0), stop=(kc == 1))
                last.then_inc(m["logits"], 1)
                pe.wait_ge(m["shared_in"], 16 * 3)

                def count():
                    pe.wait_ge(m["onehot"], 1)
                    hot = R[:, 7].rearrange("p t e -> p (t e)")
                    nc.tensor.matmul(PS[:, 3, 0:256], before[:], hot, start=True, stop=True)
                    nc.tensor.matmul(PS[:, 3, 256:512], ones[:], hot, start=True, stop=True).then_inc(m["counted"], 1)

                def up(q, b, g):
                    e = None if g is None else expert(g)
                    if not (isinstance(q, int) and q < 2):
                        pe.wait_ge(m["h"], q - 1)
                    if g is None:
                        x = [XT[:, kc, (q // 2) * P:(q // 2 + 1) * P] for kc in range(KC)]
                        w = [W13[:, kc, 16 + q % 2, :] for kc in range(KC)]
                    else:
                        pe.wait_ge(m["xT"], g + 1)
                        x = [xTs[:, b, kc, :] for kc in range(KC)]
                        w = [W13[:, kc, bass.ds(e, 1), :].rearrange("p a n -> p (a n)") for kc in range(KC)]
                    for kc in range(KC):
                        last = nc.tensor.matmul(PS[:, b, 0:2 * HID], x[kc], w[kc], start=(kc == 0), stop=(kc == 1))
                    last.then_inc(m["u"], 1)

                def expert(g):
                    at = eid[0:1, g:g + 1] if isinstance(g, int) else eid[0:1, bass.ds(g, 1)]
                    return pe.value_load(at, min_val=0, max_val=15)

                def turn_x(g, b, round4):
                    j = g % 4 if isinstance(g, int) else round4[0]
                    pe.wait_ge(m[f"xs{j}"], 16 * (g // 4 + 1) if isinstance(g, int) else round4[1])
                    if not (isinstance(g, int) and g < 2):
                        pe.wait_ge(m["xT"], g - 1)
                    for kc in range(KC):
                        last = nc.tensor.transpose(PS[:, 2 + b, kc * P:(kc + 1) * P], xs[:, j, kc * P:(kc + 1) * P], ident[:])
                    last.then_inc(m["t"], 1)

                def turn_h(q, b):
                    pe.wait_ge(m["h"], q + 1)
                    if not (isinstance(q, int) and q < 2):
                        pe.wait_ge(m["hT"], q - 1)
                    for half in range(2):
                        last = nc.tensor.transpose(PS[0:HH, 4 + b, half * P:(half + 1) * P], hb[:, b, half * HH:(half + 1) * HH], ident[:])
                    last.then_inc(m["ht"], 1)

                def down(q, b, g):
                    e = None if g is None else expert(g)
                    pe.wait_ge(m["hT"], q + 1)
                    if not (isinstance(q, int) and q < 2):
                        pe.wait_ge(m["y"], q - 1)
                    if g is None:
                        w = [W2[:, half, 16 + q % 2, :] for half in range(2)]
                    else:
                        w = [W2[:, half, bass.ds(e, 1), :].rearrange("p a n -> p (a n)") for half in range(2)]
                    for half in range(2):
                        last = nc.tensor.matmul(PS[:, 6 + b, 0:D], hT[:, b, half, :], w[half], start=(half == 0), stop=(half == 1))
                    last.then_inc(m["d"], 1)

                for q in range(NSH):
                    up(q, q % 2, None)
                    if q == NSH - 1:
                        pe.wait_ge(m["eid"], 1)
                        pe.wait_ge(m["w_in"], 16 * 3)
                        turn_x(0, 0, None)
                    if q >= 1:
                        turn_h(q - 1, 1 - q % 2)
                    if q >= 2:
                        down(q - 2, q % 2, None)
                    if q == COUNT_AT:
                        count()

                def step(g, b, turn, lag):
                    up(NSH + g, b, g)
                    if turn is not None:
                        turn_x(turn, 1 - b, lag)
                    turn_h(NSH + g - 1, 1 - b)
                    if isinstance(g, int) and g < 2:
                        down(NSH + g - 2, b, None)
                    else:
                        down(NSH + g - 2, b, g - 2)

                for g in range(4):
                    step(g, g % 2, g + 1, None)
                with pe.Fori(0, NTILE // 4 - 2) as k:
                    for j in range(4):
                        step(4 * k + 4 + j, j % 2, 4 * k + 5 + j, ((j + 1) % 4, 16 * k + 32 + (16 if j == 3 else 0)))
                for g in range(NTILE - 4, NTILE):
                    step(g, g % 2, g + 1 if g + 1 < NTILE else None, None)
                q = NSH + NTILE - 1
                turn_h(q, 1)
                down(q - 1, 0, NTILE - 2)
                down(q, 1, NTILE - 1)

            def attention1():
                layer_norm(LN[2])
                pe.wait_ge(a1["wt_in"], 64)
                pe.wait_ge(LN[2]["xt"], NT // 2)
                for i in range(4):
                    if i >= 2:
                        pe.wait_ge(a1["cT"], i - 1)
                    for kc in range(KC):
                        last = nc.tensor.matmul(PS[0:64, 4 + i % 2, :], wc[:, kc, :], XT[:, kc, i * QC:(i + 1) * QC], start=(kc == 0), stop=(kc == 1))
                    last.then_inc(a1["c_ready"], 1)
                pe.wait_ge(a1["cT"], 4)
                for i in range(2):
                    for t in range(8):
                        last = nc.tensor.transpose(PS[:, 6 + i, t * 64:(t + 1) * 64], cT[:, (8 * i + t) * P:(8 * i + t + 1) * P], ident[0:64, 0:64])
                    last.then_inc(a1["ct_turned"], 1)

                def free_x(i):
                    if not (isinstance(i, int) and i == 0):
                        pe.wait_ge(a1["x_used"], i)

                def chunk(n, b, use, kind, at):
                    free_x(x1_index(at, use, kind))
                    lo = b * SEQ + int(use[-1]) * QC
                    if use[0] == "K":
                        last = nc.tensor.matmul(psX, WK[:], cT[:, lo:lo + QC], start=True, stop=True)
                    else:
                        for kc in range(KC):
                            last = nc.tensor.matmul(psX, WQ[:, int(use[1]), kc, :], XT[:, kc, lo:lo + QC], start=(kc == 0), stop=(kc == 1))
                    last.then_inc(a1["x_ready"], 1)

                def other(n, use, kind):
                    free_x(x1_index(n, use, kind))
                    if use == "A":
                        for h in range(4):
                            for kc in range(KC):
                                at = (h * KC + kc) * 64
                                last = nc.tensor.matmul(psX[:, at:at + 64], wqn[:, h, kc * P:(kc + 1) * P], wkT[:], start=True, stop=True)
                    elif use == "V":
                        for h in range(4):
                            last = nc.tensor.matmul(psX[64 * (h % 2):64 * (h % 2) + 64, (h // 2) * D:(h // 2 + 1) * D], wvT[:], wog[:, h, :], start=True, stop=True)
                    elif use[0] == "N":
                        pair, qc = int(use[1]) // 2, int(use[1]) % 2
                        pe.wait_ge(a1["evac"], 8 * n + {"N0": 3, "N1": 4, "N2": 7, "N3": 0}[use])
                        for t in range(4):
                            last = nc.tensor.transpose(psX[:, t * P:(t + 1) * P], oq1[:, pair, 4 * qc + t].rearrange("p h c -> p (h c)"), ident[:])
                    else:
                        for t in range(2):
                            tok = (2 * int(use[1]) + t) * P
                            for pair in range(2):
                                last = nc.tensor.matmul(psX[:, t * D:(t + 1) * D], oN1[:, pair, tok:tok + P], WVO[:, pair, :], start=(pair == 0), stop=(pair == 1))
                    last.then_inc(a1["x_ready"], 1)

                def max_scores(n, par, i):
                    if not (isinstance(n, int) and n == 0 and i == 0):
                        pe.wait_ge(a1["max_taken"], 24 * n + i)
                    if i % 6 == 0:
                        pe.wait_ge(a1["hi_ready"], 10 * n + 4 + 2 * (i // 6))
                    for h, qt, at in GROUPS[i]:
                        w = (qt + 1) * P
                        q = QH[:, par, h, qt * P:(qt + 1) * P]
                        for k0 in range(0, w, QC):
                            k1 = min(w, k0 + QC)
                            diag = k1 == w
                            last = nc.tensor.matmul(psM[:, at + k0:at + k1], q, KH[:, par, k0:k1], start=True, stop=not diag)
                            if diag:
                                last = nc.tensor.matmul(psM[:, at + k1 - P:at + k1], identb[:], masks[:, 0, :], start=False, stop=True)
                        if len(GROUPS[i]) == 2 and at == 0:
                            last = nc.tensor.matmul(psM[:, at + w:at + w + P], identb[:], masks[:, 2, :], start=True, stop=True)
                    last.then_inc(a1["max_scored"], 1)

                def turn(n, par, kind, at):
                    free_x(x1_index(at, "T", kind))
                    pe.wait_ge(a1["max_taken"], 24 * n + 24)
                    nc.tensor.transpose(psX[:, 0:P], MX1[:, par, :], ident[:]).then_inc(a1["x_ready"], 1)

                def scores(n, par, s):
                    h, qc, kt = SLOTS1[s]
                    lo = first_query(qc, kt)
                    diag = kt * P >= qc * QC
                    if not (isinstance(n, int) and n == 0 and s < 3):
                        pe.wait_ge(a1["probs"], 48 * n + s - 2)
                    out = PS[:, s % 3, lo:QC]
                    keys, queries = slice(kt * P, (kt + 1) * P), slice(qc * QC + lo, (qc + 1) * QC)
                    nc.tensor.matmul(out, KH[:, par, keys], QH[:, par, h, queries], start=True, stop=False)
                    nc.tensor.matmul(out, KH[:, par, keys], QL[:, par, h, queries], start=False, stop=False)
                    nc.tensor.matmul(out, KL[:, par, keys], QH[:, par, h, queries], start=False, stop=False)
                    last = nc.tensor.matmul(out, selb[:, h, :], MR[:, par, queries], start=False, stop=not diag)
                    if diag:
                        last = nc.tensor.matmul(PS[:, s % 3, lo:lo + P], identb[:], masks[:, 1, :], start=False, stop=True)
                    last.then_inc(a1["scores"], 1)

                def values(n, b, s):
                    h, qc, kt = SLOTS1[s]
                    lo = first_query(qc, kt)
                    c = 2 * h + qc
                    pe.wait_ge(a1["probs"], 48 * n + s + 1)
                    if kt == 0 and not (isinstance(n, int) and n == 0 and c < 2):
                        pe.wait_ge(a1["evac"], 8 * n + c - 1)
                    for t in range(lo // P, 4):
                        last = nc.tensor.matmul(PS[:, 3 if qc == 0 else 6, 65 * t:65 * t + 65], PT1[:, s % 4, t * P:(t + 1) * P], CA[:, b * TB + kt, :],
                                                start=(kt == 0 and t == 0), stop=(kt == 4 * qc + 3 and t == 3))
                    last.then_inc(a1["pv"], 1)

                def step(n, b, kind, rows, w_need=None):
                    pe.wait_ge(a1[f"row{b}"], rows)
                    pe.wait_ge(a1["split"], 10 * n + 10)
                    for s in range(48):
                        scores(n, b, s)
                        if s >= 2:
                            values(n, b, s - 2)
                        for use in X1_AT[s]:
                            if has1(use, kind):
                                if use in CHUNKS:
                                    if use == "K0" and w_need is not None:
                                        pe.wait_ge(a1["w_in"], w_need)
                                    chunk(n + 1, 1 - b, use, kind, n)
                                else:
                                    other(n, use, kind)
                        if kind != 7:
                            for i in MAX1_AT[s]:
                                max_scores(n + 1, 1 - b, i)
                    values(n, b, 46)
                    values(n, b, 47)
                    if kind != 7:
                        turn(n + 1, 1 - b, kind, n)

                pe.wait_ge(a1["w_in"], 16 * 9)
                pe.wait_ge(a1["CA"], 2)
                pe.wait_ge(a1["sel"], 1)
                other(0, "A", "front")
                for use in CHUNKS:
                    chunk(0, 0, use, "front", 0)
                for i in range(len(GROUPS)):
                    max_scores(0, 0, i)
                turn(0, 0, "front", 0)
                step(0, 0, 0, 32)
                with pe.Fori(0, 3) as k:
                    step(2 * k + 1, 1, "odd", 32 * k + 32, 144 * k + 288)
                    step(2 * k + 2, 0, "even", 32 * k + 64)
                step(7, 1, 7, 128)
                for use in PREV1:
                    other(8, use, "end")

            experts(moe[0], LN[1])
            attention1()
            experts(moe[1], LN[3])


def laid_out(v):
    def heads(w, n=1):
        w = w.reshape(-1, 4, 4, 16)
        return np.pad(w, ((0, 0), (0, 0), (0, 0), (0, 16))).reshape(-1, 4, P).transpose(1, 0, 2)
    f = lambda name: np.asarray(v[name])
    wq, wk = heads(f("L0_attn_wq")), heads(f("L0_attn_wk"))
    wqk = np.stack([wq.reshape(4, KC, P, P), wk.reshape(4, KC, P, P)], 1).transpose(0, 3, 1, 2, 4).reshape(4, P, 4, P)
    out = {
        "x": f("L0_attn_x").reshape(T, D),
        "wqk": np.pad(wqk, ((0, 1), (0, 0), (0, 0), (0, 0))),
        "bqk": np.stack([heads(f("L0_attn_bq")[None])[:, 0], heads(f("L0_attn_bk")[None])[:, 0]], -1).transpose(1, 0, 2),
        "wv": f("L0_attn_wv"), "bv": f("L0_attn_bv")[None], "bo": f("L0_attn_bo")[None],
        "wo0": np.pad(f("L0_attn_wo").reshape(4, 4, 16, D), ((0, 0), (0, 0), (0, 16), (0, 0))).reshape(4, P, D),
    }
    def moe_up(l):
        w = np.concatenate([f(f"L{l}_ffn_w1"), f(f"L{l}_ffn_w3")], 1)
        a, b = f(f"L{l}_ffn_sw1").reshape(2, HID, D), f(f"L{l}_ffn_sw3").reshape(2, HID, D)
        w = np.concatenate([w, np.concatenate([a, b], 1)], 0)
        return w.reshape(NE, 2 * HID, KC, P).transpose(3, 2, 0, 1)
    def moe_down(l):
        s = f(f"L{l}_ffn_sw2").reshape(D, 2, HID).transpose(1, 0, 2)
        w = np.concatenate([f(f"L{l}_ffn_w2"), s], 0)
        return w.reshape(NE, D, 2, HH).transpose(3, 2, 0, 1)
    wqkv = f("L1_attn_Wqkv")
    q = wqkv[:, :16 * 192].reshape(D, 4, 4, 192)
    out["wqn"] = q[..., :128].transpose(1, 3, 2, 0)
    out["wqr"] = q[..., 128:].reshape(KC, P, 4, 4, 64).transpose(2, 1, 3, 0, 4)
    out["wc"] = wqkv[:, 16 * 192:].reshape(KC, P, 64).transpose(1, 0, 2)
    up = f("L1_attn_Wk_up").reshape(64, 4, 192)
    out["wkT"] = up[..., :128].transpose(1, 2, 0)
    out["wkr"] = up[..., 128:].transpose(1, 0, 2)
    out["wvT"] = f("L1_attn_Wv_up").reshape(64, 4, 128).transpose(1, 2, 0)
    out["wog"] = f("L1_attn_Wo").reshape(4, 4, 128, D).transpose(0, 2, 1, 3)
    for name in ("wqn", "wqr", "wkT", "wkr", "wvT", "wog"):
        out[name] = np.pad(out[name], ((0, 1),) + ((0, 0),) * (out[name].ndim - 1))
    out["w13"] = np.stack([moe_up(0), moe_up(1)])
    out["w2"] = np.stack([moe_down(0), moe_down(1)])
    out["gw"] = np.stack([f(f"L{l}_ffn_gate_w").reshape(16, KC, P).transpose(2, 1, 0) for l in range(2)])
    out.update(tables())
    return {k: np.ascontiguousarray(a) for k, a in out.items()}


def kernel(**inputs):
    import concourse.bacc as bacc
    from concourse.bass_utils import run_bass_kernel_spmd

    nc = bacc.Bacc("TRN2", target_bir_lowering=False, num_devices=1)
    arrays, args = {}, {}
    for name, a in laid_out(inputs).items():
        arrays[f"in_{name}_dram"] = a
        args[name] = nc.dram_tensor(f"in_{name}_dram", a.shape, mybir.dt.from_np(a.dtype), kind="ExternalInput").ap()
    args["out"] = nc.dram_tensor("out_dram", (T, D), F32, kind="ExternalOutput").ap()
    build(nc, **args)
    r = run_bass_kernel_spmd(nc, [arrays], core_ids=[0])
    return r.results[0]["out_dram"].reshape(BATCH, SEQ, D)
```

```python
from contextlib import ExitStack

import numpy as np
import concourse.bass as bass
from concourse import mybir

F32 = mybir.dt.float32
F32R = mybir.dt.float32r
BF16 = mybir.dt.bfloat16
I32 = mybir.dt.int32
U32 = mybir.dt.uint32
ALU = mybir.AluOpType
ACT = mybir.ActivationFunctionType
AXX = mybir.AxisListType.X

P = 128
D = 256
KC = D // P
BATCH = 2
SEQ = 1024
T = BATCH * SEQ
NT = T // P
TB = SEQ // P
QC = 512
EPS = 1e-5
MASKED = -1e30
COUNT_AT = 5
SBUF = 229376

UNITS = [(0, kt) for kt in range(4)] + [(1, kt) for kt in range(8)]
BANKS = [[(3, 0, 4)], [(0, 0, 1), (2, 0, 3)], [(5, 0, 4)], [(5, 4, 2), (1, 0, 2)], [(4, 0, 4)], [(4, 4, 1), (6, 4, 3)],
         [(6, 0, 4)], [(7, 0, 4)], [(7, 4, 4)]]
NB = len(BANKS)
MAXES = 4 * NB
BLOCK_OF = [qt for bank in BANKS for qt, _, n in bank for _ in range(n)]
PARTIAL_AT = [BLOCK_OF.index(qt) for qt in range(TB)]


def first_query(qc, kt):
    return max(0, kt * P - qc * QC)


def wide(lo):
    return min(lo, QC - 256)


def tables():
    t = np.arange(SEQ, dtype=np.float32)
    start = 2.0 ** (-8.0 / 16)
    slopes = np.asarray([start * start ** i for i in range(16)], np.float32)
    four = slopes * np.float32(4)
    hi = (four.view(np.uint32) & np.uint32(0xFFFFF000)).view(np.float32)
    lo = four - hi
    coef = np.zeros((P, 4, 4), np.float32)
    for g in range(4):
        for h in range(4):
            a, b, r = hi[4 * g + h], lo[4 * g + h], 32 * h + 16
            coef[r, g] = (0, -a, 1, 0)
            coef[r + 1, g] = (1, 0, 0, a)
            coef[r + 2, g] = (0, -b, 1, 0)
            coef[r + 3, g] = (b, 0, 0, 1)
            coef[r + 4, g] = (0, 0, 1, 0)
    inv = (np.float32(1) / np.power(np.float32(10000), np.arange(0, 64, 2, dtype=np.float32) / np.float32(64)))
    ang = np.outer(inv.astype(np.float32), t).astype(np.float32)
    rope = np.zeros((P, 2, SEQ), np.float32)
    rope[64:96, 0] = rope[96:128, 0] = np.cos(ang)
    rope[64:96, 1] = np.sin(ang)
    rope[96:128, 1] = -np.sin(ang)
    i = np.arange(P)
    masks = np.zeros((P, 2, P), np.float32)
    masks[:, 0] = np.where(i[None, :] > i[:, None], MASKED, 0)
    masks[:, 1] = np.where(i[:, None] > i[None, :], MASKED, 0)
    spread = np.zeros((P, P), np.float32)
    for h in range(4):
        spread[32 * h + 16, 32 * h:32 * h + 32] = 1
    before = (i[:, None] < i[None, :]).astype(np.float32)
    e = np.arange(16, dtype=np.float32)
    small = np.zeros((1, 16 + 16 * 16 + NTILE * 16), np.float32)
    small[:, 0:16] = 16 - e
    small[:, 16:272] = (e[None, :] < e[:, None]).astype(np.float32).reshape(1, 256)
    small[:, 272:] = np.repeat(np.arange(NTILE, dtype=np.float32), 16)[None]
    return {
        "c_sel": np.repeat((np.arange(P)[:, None] % 4 == np.arange(4)[None]) & (np.arange(P)[:, None] < 8), P, 1).reshape(P, 4, P).astype(np.float32),
        "c_ident": np.eye(P, dtype=np.float32), "c_masks": masks, "c_spread": spread, "c_before": before,
        "c_pos": t.reshape(1, SEQ), "c_coef": coef, "c_rope": rope, "c_small": small,
    }


SCALE1 = float(1.0 / np.sqrt(192.0))
NTILE = 48
NE = 18
HID = 176
HH = HID // 2
W13_BYTES = KC * NE * 2 * HID * 4
NTAIL = 4
NSH = 2 * NT - NTAIL
STEPS = NSH + NTILE + NTAIL


class Count:

    def __init__(self, sem):
        self.sem, self.n = sem, 0

    def up(self, ins):
        self.n += 1
        ins.then_inc(self.sem, 1)
        return self.n


def build(nc, **A):
    ctx = ExitStack()
    with ctx:
        def sb(name, shape, dt=F32):
            return ctx.enter_context(nc.sbuf_tensor(name, shape, dt))

        def sem(name):
            return ctx.enter_context(nc.semaphore(name))

        X = sb("X", [P, NT, D])
        XT = sb("XT", [P, KC, T])
        stats = sb("stats", [P, NT, 6])
        mv = sb("mv", [P, NT, 2])
        rs = sb("rs", [P, 4, NT])
        ident = sb("ident", [P, P])
        identb = sb("identb", [P, P], BF16)
        masks = sb("masks", [P, 2, P], BF16)
        spread = sb("spread", [P, P])
        coef = sb("coef", [P, 4, 4])
        bqk = sb("bqk", [P, 4, 2])
        cg = sb("cg", [P, 2, 4])
        before = sb("before", [P, P])
        ones = sb("ones", [P, P])
        small = sb("small", [P, 16 + 256 + NTILE * 16])
        zeros = sb("zeros", [P, D])
        arena = nc.sbuf_base

        class Phase:

            def __init__(self):
                self.at = arena + 64 - arena % 64

            def __call__(self, name, shape, dt=F32):
                size = int(np.prod(shape[1:])) * (2 if dt == BF16 else 4)
                assert self.at + size <= SBUF, (name, self.at + size)
                t = nc.alloc_sbuf_tensor_at(name, shape, dt, offset=self.at)
                self.at += (size + 63) // 64 * 64
                return t

        XN = Phase()("XN", [P, NT, D])
        arena += NT * D * 4
        ph = Phase()
        wqk = ph("wqk", [P, 4, P])
        wo0 = ph("wo0", [P, 4, D])
        wv = ph("wv", [P, KC, D])
        bob = ph("bob", [P, D])
        bvb = ph("bvb", [P, D])
        pos = ph("pos", [P, SEQ])
        masksf = ph("masksf", [P, 2, P])
        V = ph("V", [P, NT, D])
        VS = ph("VS", [P, 2, TB, 4, 32])
        tq = ph("tq", [P, 2, QC])
        QKs = ph("QKs", [P, 4, SEQ], F32R)
        QS = ph("QS", [P, 2, 4, SEQ], F32R)
        KS = ph("KS", [P, 2, 4, SEQ], F32R)
        PT = ph("PT", [P, 3, 2, QC])
        MX = ph("MX", [P, 2, P])
        MXP = ph("MXP", [P, 4, 4 * NB])
        mneg = ph("mneg", [32, P])
        mh = ph("mh", [32, 2, P], F32R)
        oT = ph("oT", [P, QC])
        rc = ph("rc", [P, 16])
        rb = ph("rb", [P, 16, 32])
        oN = ph("oN", [P, QC])

        pa = Phase()
        pa.at -= NT * D * 4
        KH = pa("KH", [P, 2, SEQ], F32R)
        KL = pa("KL", [P, 2, SEQ], F32R)
        cT = pa("cT", [64, T])
        CA = pa("CA", [P, NT, 65])
        wc = pa("wc", [P, KC, 64])
        wqn = pa("wqn", [P, 4, D])
        wkT = pa("wkT", [P, 64])
        WQ = pa("WQ", [P, 4, KC, P])
        WK = pa("WK", [64, P])
        wog = pa("wog", [P, 4, D])
        wvT = pa("wvT", [P, 64])
        WVO = pa("WVO", [P, 2, D])
        rope = pa("rope", [P, 2, SEQ])
        self_ = pa("self_", [P, 4, P])
        selb = pa("selb", [P, 4, P], BF16)
        MR = pa("MR", [P, 2, SEQ], BF16)
        assert pa.at <= arena + 64 + W13_BYTES
        QH = pa("QH", [P, 2, 4, SEQ], F32R)
        QL = pa("QL", [P, 2, 4, SEQ], F32R)
        r1 = pa("r1", [P, 2, QC])
        r2 = pa("r2", [P, 2, QC])
        F = pa("F", [P, 2, QC])
        PT1 = pa("PT1", [P, 4, QC])
        rc1 = pa("rc1", [P, 2, 4])
        rt1 = pa("rt1", [P, 1])
        oq1 = pa("oq1", [P, 2, TB, 2, 64])
        MX1 = pa("MX1", [P, 2, P])
        MXP1 = pa("MXP1", [P, 4, 4 * NB])
        mn1 = pa("mn1", [32, 2, P])
        mb1 = pa("mb1", [32, 2, P], BF16)
        oN1 = pa("oN1", [P, 2, SEQ])
        pm = Phase()
        W13 = pm("W13", [P, KC, NE, 2 * HID])
        W2 = pm("W2", [HH, 2, NE, D])
        gw = pm("gw", [P, KC, 16])
        xs = pm("xs", [P, 4, D])
        xTs = pm("xTs", [P, 2, KC, P])
        sg = pm("sg", [P, 2, HID])
        hb = pm("hb", [P, 2, HID])
        hT = pm("hT", [HH, 2, 2, P])
        ys = pm("ys", [P, 2, D])
        yg = pm("yg", [P, 4, 2, D])
        R = pm("R", [P, 8, NT, 16])
        rt = pm("rt", [P, 8, NT])
        carry = pm("carry", [P, NT + 1, 16])
        tl = pm("tl", [P, 4, 16])
        tli = pm("tli", [P, 16], I32)
        owner = pm("owner", [P, NTILE, 16])
        lt = pm("lt", [P, 16, 16])
        eidf = pm("eidf", [P, NTILE])
        eid = pm("eid", [P, NTILE], I32)
        slot = pm("slot", [P, 2, NT], U32)
        slots = nc.dram_tensor("slots", [NTILE * P, D], F32, kind="Internal").ap()
        outs = nc.dram_tensor("outs", [NTILE * P, D], F32, kind="Internal").ap()
        PS = ctx.enter_context(nc.psum_tensor("PS", [P, 8, QC], F32))
        psO = PS[:, 6, :]
        psX = PS[:, 7, :]

        const_in = sem("const_in"); x_in = [sem(f"x_in{i}") for i in range(4)]; ident_in = sem("ident_in"); w_in = sem("w_in")
        consts_made = sem("consts_made")
        dve_done = sem("dve_done")
        dv = Count(dve_done)
        out_done = sem("out_done")
        pool_ready = sem("pool_ready")
        LN = [{k: sem(f"ln{n}_{k}") for k in ("var", "sd", "xn", "t", "xt")} for n in range(4)]
        v_ready = sem("v_ready"); v_taken = sem("v_taken"); bo_added = sem("bo_added")
        coef_ready = sem("coef_ready")
        a0 = {k: sem("a0_" + k) for k in (
            "scores", "probs", "pv", "max_scored", "max_taken", "maxed", "x_ready", "x_used", "hi_ready",
            "split", "neg", "neg_hi", "evac", "normed", "staged", "w_in", "row0", "row1", "recip", "cg")}
        copied = [[sem(f"a0_copied{p}{h}") for h in range(4)] for p in range(2)]

        moe = [{k: sem(f"m{n}_{k}") for k in (
            "w_in", "gate_in", "shared_in", "logits", "shifted", "exps", "onehot", "counted", "eid", "slot", "scattered",
            "u", "sg", "h", "ht", "hT", "d", "y", "t", "xT", "xs0", "xs1", "xs2", "xs3", "stored0", "stored1",
            "got0", "got1", "got2", "got3", "added")} for n in range(2)]
        a1 = {k: sem("a1_" + k) for k in (
            "scores", "probs", "pv", "max_scored", "max_taken", "maxed", "x_ready", "x_used", "plain", "roped", "summed", "hi_ready",
            "split", "neg", "neg_mid", "evac", "recip", "w_in", "wt_in", "row0", "row1", "made", "sel", "c_ready", "cT", "ct_turned", "CA")}
        zero_made = sem("zero_made"); zero_in = sem("zero_in")
        block = ctx.enter_context(nc.Block())

        FRONT = ["P0", "P1", "P2", "P3"]
        PREV = ["S1", "B1", "W1a", "W1b"]
        OWN = ["S0", "B0", "W0a", "W0b"]
        ORDERS = {"front": FRONT + ["T"], 0: FRONT + OWN + ["T"], 1: FRONT + PREV + OWN + ["T"], 7: PREV + OWN, "end": PREV}

        def x_index(n, use, kind):
            at = ORDERS[kind].index(use)
            if kind == "front":
                return at
            if kind == 0:
                return 5 + at
            base = 14
            if kind == 1:
                return (n - 1) * 13 + (base + at)
            return base + 6 * 13 + at + (8 if kind == "end" else 0)

        CHUNKS = ["K0", "K1", "Q00", "Q01", "Q10", "Q11", "Q20", "Q21", "Q30", "Q31"]
        X1_AT = {s: [] for s in range(-1, 48)}
        for at, use in ((-1, "K0"), (-1, "K1"), (2, "A"), (2, "Q00"), (4, "N3"), (5, "Q01"), (6, "O0"), (7, "O1"), (8, "O2"), (9, "O3"),
                        (11, "Q10"), (13, "Q11"), (16, "Q20"), (18, "Q21"), (20, "Q30"), (22, "Q31"), (24, "V"), (28, "N0"),
                        (30, "N1"), (45, "N2")):
            X1_AT[at].append(use)
        MAX1_AT = [[] for _ in range(48)]
        for i in range(MAXES):
            MAX1_AT[10 + i * 36 // MAXES].append(i)
        HI_AT = {}
        for s in range(-1, 48):
            for use in X1_AT[s]:
                if use in CHUNKS:
                    HI_AT.setdefault(s + 2 if use not in ("K0", "K1") else s + 1, []).append(use)
        SLOTS1 = [(h, qc, kt) for h in range(4) for qc, kt in UNITS]
        FRONT_MAX = {use: list(range(NB * i, NB * (i + 1))) for i, use in enumerate(("Q11", "Q21", "Q31"))}
        TURN_BEHIND = "Q01"
        PREV1 = ["N3", "O0", "O1", "O2", "O3"]
        ALL1 = [u for s in range(-1, 48) for u in X1_AT[s]]
        FRONT1 = ["A"] + CHUNKS

        def has1(use, kind):
            if kind == "end":
                return use in PREV1
            if use in PREV1:
                return kind != 0
            if use in CHUNKS:
                return kind != 7
            if use == "A":
                return kind == "odd"
            if use == "V":
                return kind in (0, "even")
            return True

        ORDERS1 = {kind: [u for u in ALL1 if has1(u, kind)] + (["T"] if kind != 7 else []) for kind in (0, "odd", "even", 7)}
        ORDERS1["front"] = FRONT1 + ["T"]
        ORDERS1["end"] = PREV1
        FULL1 = len(ORDERS1["odd"])
        BASE1 = len(ORDERS1["front"]) + len(ORDERS1[0])
        assert FULL1 == len(ORDERS1["even"])

        def x1_index(n, use, kind):
            at = ORDERS1[kind].index(use)
            if kind == "front":
                return at
            if kind == 0:
                return len(ORDERS1["front"]) + at
            if kind in ("odd", "even"):
                return (n - 1) * FULL1 + (BASE1 + at)
            return BASE1 + 6 * FULL1 + at + (len(ORDERS1[7]) if kind == "end" else 0)


        def x1_bank(use, kind):
            return PS[:, 3, :] if kind == "front" and use in CHUNKS[::2] else psX

        X_AT = {-1: "P0", 0: "P1", 1: "P2", 2: "P3", 3: "S1", 5: "B1", 7: "W1a", 9: "W1b", 13: "S0", 15: "B0", 17: "W0a", 19: "W0b"}
        MAX_AT = [[] for _ in range(24)]
        for i in range(MAXES):
            MAX_AT[7 + i * 16 // MAXES].append(i)
        SLOTS = [(qc, kt, pair) for qc, kt in UNITS for pair in range(2)]

        @block.sync
        def _(sp):
            sp.dma_start(ident[:], A["c_ident"]).then_inc(ident_in, 16)
            for i in range(4):
                sp.dma_start(X[:, 4 * i:4 * i + 4, :], A["x"].rearrange("(t p) d -> p t d", p=P)[:, 4 * i:4 * i + 4, :]).then_inc(x_in[i], 16)
            sp.dma_start(masksf[:], A["c_masks"]).then_inc(const_in, 16)
            sp.dma_start(spread[:], A["c_spread"]).then_inc(const_in, 16)
            sp.dma_start(coef[:], A["c_coef"]).then_inc(const_in, 16)
            sp.dma_start(bqk[:], A["bqk"]).then_inc(const_in, 16)
            sp.dma_start(pos[:], A["c_pos"].to_broadcast([P, SEQ])).then_inc(const_in, 16)
            sp.dma_start(before[:], A["c_before"]).then_inc(const_in, 16)
            sp.dma_start(small[:], A["c_small"].to_broadcast([P, 16 + 256 + NTILE * 16])).then_inc(const_in, 16)
            sp.dma_start(bvb[:], A["bv"].to_broadcast([P, D])).then_inc(w_in, 16)
            sp.dma_start(bob[:], A["bo"].to_broadcast([P, D])).then_inc(w_in, 16)
            sp.dma_start(wv[:], A["wv"].rearrange("(c p) n -> p c n", p=P)).then_inc(w_in, 16)
            sp.dma_start(wo0[:], A["wo0"].rearrange("g p n -> p g n")).then_inc(w_in, 16)
            sp.dma_start(wqk[:], A["wqk"][0]).then_inc(a0["w_in"], 16)

            STACK_ORDER = ((0, 0), (1, 0), (0, 1), (1, 1), (2, 0), (2, 1), (3, 0), (3, 1))

            def stack(n, par):
                sp.wait_ge(a0["split"], 4 * n + 2)
                for h, side in STACK_ORDER:
                    if (h, side) == (0, 1):
                        sp.wait_ge(a0["split"], 4 * n + 4)
                    dst, src = ((QS, (0, 0, 1, 1)), (KS, (2, 3, 2, 3)))[side]
                    for quarter in range(4):
                        sp.dma_start(dst[32 * quarter:32 * quarter + 32, par, h, :].bitcast(F32), QKs[32 * h:32 * h + 32, src[quarter], :].bitcast(F32)).then_inc(copied[par][h], 16)

            def neg_rows(n, par):
                sp.wait_ge(a0["neg"], n + 1)
                for part in range(2):
                    sp.dma_start(QS[20 + 64 * part:21 + 64 * part, par, :, :].rearrange("o h t -> o (h t)").bitcast(F32), mh[:, part, :].bitcast(F32)).then_inc(a0[f"row{par}"], 16)

            stack(0, 0)
            neg_rows(0, 0)
            stack(1, 1)
            sp.wait_ge(a0["x_ready"], x_index(0, "P3", 0) + 1)
            sp.dma_start(wqk[:], A["wqk"][1]).then_inc(a0["w_in"], 16)
            neg_rows(1, 1)
            with sp.Fori(0, 3) as k:
                stack(2 * k + 2, 0)
                neg_rows(2 * k + 2, 0)
                stack(2 * k + 3, 1)
                g = sp.snap(k + 2)
                sp.wait_ge(a0["x_ready"], x_index(2 * k + 2, "P3", 1) + 1)
                sp.dma_start(wqk[:], A["wqk"][bass.ds(g, 1)].rearrange("a p b c -> p (a b) c")).then_inc(a0["w_in"], 16)
                neg_rows(2 * k + 3, 1)
            sp.wait_ge(a0["w_in"], 16 * 5)
            sp.wait_ge(zero_made, 1)
            sp.dma_start(slots.rearrange("(g p) d -> p g d", p=P), zeros[:, None, :].to_broadcast([P, NTILE, D])).then_inc(zero_in, 16)

            def experts(m, layer):
                sp.dma_start(gw[:], A["gw"][layer]).then_inc(m["gate_in"], 16)
                for kc in range(KC):
                    sp.dma_start(W13[:, kc, 16:18], A["w13"][layer, :, kc, 16:18]).then_inc(m["shared_in"], 16)
                sp.dma_start(W2[:, :, 16:18], A["w2"][layer, :, :, 16:18]).then_inc(m["shared_in"], 16)
                for kc in range(KC):
                    sp.dma_start(W13[:, kc, 0:16], A["w13"][layer, :, kc, 0:16]).then_inc(m["w_in"], 16)
                sp.dma_start(W2[:, :, 0:16], A["w2"][layer, :, :, 0:16]).then_inc(m["w_in"], 16)

                def load(g, j):
                    if not isinstance(g, int):
                        sp.wait_ge(m["t"], g - 3)
                    src = slots.rearrange("(g p) d -> p g d", p=P)
                    src = src[:, g:g + 1, :] if isinstance(g, int) else src[:, bass.ds(g, 1), :]
                    sp.dma_start(xs[:, j:j + 1, :], src).then_inc(m[f"xs{j}"], 16)

                def store(g, j):
                    sp.wait_ge(m["y"], NSH + g + 1)
                    dst = outs.rearrange("(g p) d -> p g d", p=P)
                    dst = dst[:, g:g + 1, :] if isinstance(g, int) else dst[:, bass.ds(g, 1), :]
                    sp.dma_start(dst, ys[:, j:j + 1, :]).then_inc(m[f"stored{j}"], 16)

                sp.wait_ge(m["scattered"], 16 * 2 * NT)
                for g in range(4):
                    load(g, g)
                with sp.Fori(0, NTILE // 4 - 1) as k:
                    for j in range(4):
                        load(4 * k + 4 + j, j)
                        store(4 * k + j, j % 2)
                for j in range(4):
                    store(NTILE - 4 + j, j % 2)

            sp.wait_ge(a0["x_used"], x_index(8, "W1b", "end") + 1)
            def attention1():
                def group_weights(g):
                    pick = (lambda name: A[name][g]) if isinstance(g, int) else (lambda name: A[name][bass.ds(g, 1)].rearrange(
                        "a p b c -> p (a b) c" if name in ("wqn", "wog") else "a p b c d -> p (a b) c d" if name == "wqr" else "a p b -> p (a b)"))
                    sp.dma_start(wqn[:], pick("wqn")).then_inc(a1["w_in"], 16)
                    sp.dma_start(wkT[:], pick("wkT")).then_inc(a1["w_in"], 16)
                    for h in range(4):
                        src = A["wqr"][g, :, h] if isinstance(g, int) else A["wqr"][bass.ds(g, 1), :, h].rearrange("a p b c -> p (a b) c")
                        sp.dma_start(WQ[:, h, :, 64:128], src).then_inc(a1["w_in"], 16)
                    sp.dma_start(WK[:, 64:128], pick("wkr")).then_inc(a1["w_in"], 16)
                    sp.dma_start(wog[:], pick("wog")).then_inc(a1["w_in"], 16)
                    sp.dma_start(wvT[:], pick("wvT")).then_inc(a1["w_in"], 16)

                sp.dma_start(wc[:], A["wc"]).then_inc(a1["wt_in"], 16)
                sp.dma_start(rope[:], A["c_rope"]).then_inc(a1["wt_in"], 16)
                sp.dma_start(self_[:], A["c_sel"]).then_inc(a1["wt_in"], 16)
                sp.dma_start(WK[:, 0:64], A["c_ident"][0:64, 0:64]).then_inc(a1["wt_in"], 16)
                group_weights(0)

                def neg_rows(n, par):
                    sp.wait_ge(a1["neg"], n + 1)
                    for part in range(2):
                        sp.dma_start(MR[4 * part:4 * part + 4, par, :], mb1[:, part, :]).then_inc(a1[f"row{par}"], 16)

                sp.wait_ge(a1["made"], 3)
                neg_rows(0, 0)
                sp.wait_ge(a1["x_ready"], x1_index(0, "V", 0) + 1)
                group_weights(1)
                neg_rows(1, 1)
                with sp.Fori(0, 3) as k:
                    neg_rows(2 * k + 2, 0)
                    g = sp.snap(k + 2)
                    sp.wait_ge(a1["x_ready"], x1_index(2 * k + 2, "V", "even") + 1)
                    group_weights(g)
                    neg_rows(2 * k + 3, 1)
                sp.wait_ge(a1["w_in"], 16 * 9 * 5)

            experts(moe[0], 0)
            sp.wait_ge(moe[0]["u"], STEPS)
            attention1()
            sp.wait_ge(a1["x_used"], x1_index(8, "O3", "end") + 1)
            experts(moe[1], 1)
            for i in range(4):
                sp.wait_ge(moe[1]["added"], 2 * (4 * i + 4))
                sp.dma_start(A["out"].rearrange("(t p) d -> p t d", p=P)[:, 4 * i:4 * i + 4, :], X[:, 4 * i:4 * i + 4, :]).then_inc(out_done, 16)
            sp.wait_ge(out_done, 64)
            sp.wait_ge(zero_in, 16)

        @block.gpsimd
        def _(pool):
            nc.gpsimd.memset(VS[:], 0.0).then_inc(pool_ready, 1)
            pool.wait_ge(pool_ready, 1)
            nc.gpsimd.memset(VS[:, :, :, :, 16:17].rearrange("p a b h o -> p (a b h) o"), 1.0).then_inc(pool_ready, 1)
            pool.wait_ge(w_in, 64)
            pool.wait_ge(LN[0]["xn"], NT)
            nc.gpsimd.tensor_tensor(X[:], X[:], bob[:, None, :].to_broadcast([P, NT, D]), ALU.add).then_inc(bo_added, 1)
            pool.wait_ge(v_taken, NT // 2)
            pool.wait_ge(pool_ready, 2)

            def stage(n, g, b):
                for kt in range(TB):
                    src = V[:, b * TB + kt, bass.ds(g * 64, 64)] if not isinstance(g, int) else V[:, b * TB + kt, g * 64:g * 64 + 64]
                    last = nc.gpsimd.tensor_copy(VS[:, b, kt, :, 0:16], src.rearrange("p (h d) -> p h d", h=4))
                last.then_inc(a0["staged"], 1)

            stage(0, 0, 0)
            stage(1, 0, 1)
            with pool.Fori(0, 3) as k:
                g = pool.snap(k + 1)
                pool.wait_ge(a0["pv"], 24 * (2 * k + 1))
                pool.wait_ge(pool_ready, 2)
                stage(2 * k + 2, g, 0)
                pool.wait_ge(a0["pv"], 24 * (2 * k + 2))
                pool.wait_ge(pool_ready, 2)
                stage(2 * k + 3, g, 1)

            def route(m, after=None):
                pool.wait_ge(zero_in, 16)
                for j in range(2):
                    pool.wait_ge(m["slot"], j + 1)
                    for i in range(NT):
                        nc.gpsimd.indirect_dma_start(slots, bass.IndirectOffsetOnAxis(slot[:, j, i:i + 1], 0), XN[:, i, :], None).then_inc(m["scattered"], 16)
                for j in range(2):
                    pool.wait_ge(m[f"stored{j}"], 16 * NTILE // 2)
                for i in range(NT):
                    if i >= 4:
                        pool.wait_ge(m["added"], 2 * (i - 3))
                    for j in range(2):
                        nc.gpsimd.indirect_dma_start(yg[:, i % 4, j, :], None, outs, bass.IndirectOffsetOnAxis(slot[:, j, i:i + 1], 0)).then_inc(m[f"got{i % 4}"], 16)
                if after:
                    after()

            def attention1_constants():
                pool.wait_ge(moe[0]["u"], STEPS)
                nc.gpsimd.memset(MR[:], 0.0).then_inc(a1["made"], 1)
                nc.gpsimd.memset(CA[:, :, 64:65], 1.0).then_inc(a1["made"], 1)

            def attention1():
                pool.wait_ge(moe[0]["added"], 2 * NT)
                nc.gpsimd.memset(r2[:], 0.0).then_inc(a1["made"], 1)
                pool.wait_ge(a1["made"], 3)

                def chunk(c, par, use):
                    b = CHUNKS.index(use) % 2
                    lo = int(use[-1]) * QC
                    low = KL[:, par, lo:lo + QC] if use[0] == "K" else QL[:, par, int(use[1]), lo:lo + QC]
                    high = KH[:, par, lo:lo + QC] if use[0] == "K" else QH[:, par, int(use[1]), lo:lo + QC]
                    pool.wait_ge(a1["plain"], c + 1)
                    pool.wait_ge(a1["roped"], c + 1)
                    nc.gpsimd.tensor_tensor(F[:, b, :], r1[:, b, :], r2[:, b, :], ALU.add).then_inc(a1["summed"], 1)
                    pool.wait_ge(a1["hi_ready"], c + 1)
                    nc.gpsimd.tensor_tensor(low, F[:, b, :], high.bitcast(F32), ALU.subtract).then_inc(a1["split"], 1)

                def front(n, par):
                    for i, use in enumerate(CHUNKS):
                        chunk(10 * n + i, par, use)

                front(0, 0)
                front(1, 1)
                with pool.Fori(0, 3) as k:
                    front(2 * k + 2, 0)
                    front(2 * k + 3, 1)

            route(moe[0], attention1_constants)
            attention1()
            route(moe[1])

        @block.scalar
        def _(act):
            def layer_norm(ln, groups=1, behind=None):
                for g in range(groups):
                    tiles = slice(g * NT // groups, (g + 1) * NT // groups)
                    act.wait_ge(ln["var"], g + 1)
                    nc.scalar.activation(rs[:, 1, tiles], rs[:, 0, tiles], ACT.Sqrt).then_inc(ln["sd"], 1)
                    for i in range(tiles.start // 2, tiles.stop // 2):
                        act.wait_ge(ln["t"], i + 1)
                        nc.scalar.activation(XT[:, :, 2 * i * P:(2 * i + 2) * P], PS[:, i % 4, :].rearrange("p (c t) -> p c t", c=KC),
                                             ACT.Copy).then_inc(ln["xt"], 1)
                    if behind:
                        behind(g)

            layer_norm(LN[0], 4)

            def probs(n, s, wait_free):
                qc, kt, pair = SLOTS[s]
                lo = first_query(qc, kt)
                act.wait_ge(a0["scores"], 24 * n + s + 1)
                if wait_free:
                    act.wait_ge(a0["pv"], 24 * n + s - 2)
                nc.scalar.activation(PT[:, s % 3, :, lo:QC], PS[:, 2 * (s % 2):2 * (s % 2) + 2, lo:QC], ACT.Exp,
                                     scale=0.25).then_inc(a0["probs"], 1)

            def high_part(n, i, par, kind, at):
                side, c = i // 2, i % 2
                act.wait_ge(a0["x_used"], x_index(at, f"P{i}", kind) + 1)
                bias = cg[:, par, 2 * side:2 * side + 1]
                nc.scalar.activation(QKs[:, 2 * side, c * QC:(c + 1) * QC], tq[:, i % 2, :], ACT.Identity, bias=bias).then_inc(a0["hi_ready"], 1)

            def evac(n, qc, kind):
                act.wait_ge(a0["pv"], 24 * n + (8 if qc == 0 else 24))
                if not (kind == 0 and qc == 0):
                    if qc == 0:
                        act.wait_ge(a0["x_used"], x_index(n, "B1", kind) + 1)
                    else:
                        act.wait_ge(a0["x_used"], x_index(n, "B0", kind) + 1)
                nc.scalar.activation(oT[:], psO, ACT.Copy).then_inc(a0["evac"], 1)

            def step(n, b, kind):
                for s in range(-1, 24):
                    if s >= 0:
                        probs(n, s, not (isinstance(n, int) and n == 0 and s < 3))
                    if kind != 7 and X_AT.get(s, "")[:1] == "P":
                        high_part(n + 1, int(X_AT[s][1]), 1 - b, kind, n)
                    if s == 10:
                        evac(n, 0, kind)
                evac(n, 1, kind)

            for i in range(4):
                high_part(0, i, 0, "front", 0)
            step(0, 0, 0)
            with act.Fori(0, 3) as k:
                step(2 * k + 1, 1, 1)
                step(2 * k + 2, 0, 1)
            step(7, 1, 7)

            def experts(m, ln):
                layer_norm(ln, 2)
                act.wait_ge(m["shifted"], 1)
                nc.scalar.activation(R[:, 1], R[:, 0], ACT.Exp).then_inc(m["exps"], 1)

                def silu(q, b, c):
                    act.wait_ge(m["u"], q + 1)
                    if c:
                        act.wait_ge(m["h"], q - 1)
                    nc.scalar.activation(sg[:, b, :], PS[:, b, 0:HID], ACT.Silu).then_inc(m["sg"], 1)

                def turned_x(g, b, c):
                    act.wait_ge(m["t"], g + 1)
                    if c:
                        act.wait_ge(m["u"], NSH + g - 1)
                    nc.scalar.activation(xTs[:, b], PS[:, 2 + b, 0:D].rearrange("p (c t) -> p c t", c=KC), ACT.Copy).then_inc(m["xT"], 1)

                def turned_h(q, b, c):
                    act.wait_ge(m["ht"], q + 1)
                    if c:
                        act.wait_ge(m["d"], q - 1)
                    nc.scalar.activation(hT[:, b], PS[0:HH, 4 + b, 0:2 * P].rearrange("p (c t) -> p c t", c=2), ACT.Copy).then_inc(m["hT"], 1)

                def step(q, g, b, c):
                    silu(q, b, c or q >= 2)
                    if g is not None:
                        turned_x(g, 1 - b, c or g >= 2)
                    if c or q >= 1:
                        turned_h(q - 1, 1 - b, c or q >= 3)

                for q in range(NSH):
                    step(q, 0 if q == NSH - 1 else None, q % 2, False)
                step(NSH, 1, 0, False)
                step(NSH + 1, 2, 1, False)
                with act.Fori(0, NTILE // 2 - 2) as k:
                    step(NSH + 2 + 2 * k, 2 * k + 3, 0, True)
                    step(NSH + 3 + 2 * k, 2 * k + 4, 1, True)
                q = NSH + NTILE - 2
                step(q, NTILE - 1, 0, False)
                step(q + 1, None, 1, False)
                for q in range(NSH + NTILE, STEPS):
                    step(q, None, q % 2, True)
                turned_h(STEPS - 1, 1, True)

            experts(moe[0], LN[1])

            def attention1():
                def latent(i):
                    act.wait_ge(a1["c_ready"], i + 1)
                    nc.scalar.activation(cT[:, i * QC:(i + 1) * QC], PS[0:64, 4 + i % 2, :], ACT.Copy).then_inc(a1["cT"], 1)

                layer_norm(LN[2], 4, latent)
                def plain(n, use, kind, at):
                    i = CHUNKS.index(use)
                    c = 10 * n + i
                    act.wait_ge(a1["x_ready"], x1_index(at, use, kind) + 1)
                    if not (isinstance(c, int) and c < 2):
                        act.wait_ge(a1["summed"], c - 1)
                    nc.scalar.activation(r1[0:64, i % 2, :], x1_bank(use, kind)[0:64, :], ACT.Copy).then_inc(a1["plain"], 1)

                def high_part(n, use, par):
                    i = CHUNKS.index(use)
                    c = 10 * n + i
                    lo = int(use[-1]) * QC
                    high = KH[:, par, lo:lo + QC] if use[0] == "K" else QH[:, par, int(use[1]), lo:lo + QC]
                    act.wait_ge(a1["summed"], c + 1)
                    nc.scalar.activation(high, F[:, i % 2, :], ACT.Copy).then_inc(a1["hi_ready"], 1)

                def probs(n, s):
                    h, qc, kt = SLOTS1[s]
                    lo = first_query(qc, kt)
                    act.wait_ge(a1["scores"], 48 * n + s + 1)
                    if not (isinstance(n, int) and n == 0 and s < 4):
                        act.wait_ge(a1["pv"], 48 * n + s - 3)
                    nc.scalar.activation(PT1[:, s % 4, lo:QC], PS[:, s % 3, lo:QC], ACT.Exp, scale=SCALE1).then_inc(a1["probs"], 1)

                def turned(n, use, kind):
                    pair, qc = int(use[1]) // 2, int(use[1]) % 2
                    act.wait_ge(a1["x_ready"], x1_index(n, use, kind) + 1)
                    nc.scalar.activation(oN1[:, pair, qc * QC:(qc + 1) * QC], psX, ACT.Copy).then_inc(a1["x_used"], 1)

                def step(n, b, kind):
                    for s in range(-1, 48):
                        if s >= 0:
                            probs(n, s)
                        for use in X1_AT[s]:
                            if use[0] == "N" and has1(use, kind):
                                turned(n, use, kind)
                        if kind != 7:
                            for use in HI_AT.get(s, ()):
                                high_part(n + 1, use, 1 - b)
                            for use in X1_AT[s]:
                                if use in CHUNKS:
                                    plain(n + 1, use, kind, n)

                for i, use in enumerate(CHUNKS):
                    plain(0, use, "front", 0)
                    if i >= 1:
                        high_part(0, CHUNKS[i - 1], 0)
                    if use == TURN_BEHIND:
                        for j in range(2):
                            act.wait_ge(a1["ct_turned"], j + 1)
                            nc.scalar.activation(CA[:, 8 * j:8 * j + 8, 0:64], PS[:, j, :].rearrange("p (t c) -> p t c", c=64), ACT.Copy).then_inc(a1["CA"], 1)
                high_part(0, CHUNKS[-1], 0)
                step(0, 0, 0)
                with act.Fori(0, 3) as k:
                    step(2 * k + 1, 1, "odd")
                    step(2 * k + 2, 0, "even")
                step(7, 1, 7)
                turned(8, "N3", "end")

            attention1()
            experts(moe[1], LN[3])

        @block.vector
        def _(dve):
            def link(ins):
                dve.wait_ge(dve_done, dv.up(ins))

            def constants():
                dve.wait_ge(ident_in, 16)
                dve.wait_ge(const_in, 112)
                nc.vector.tensor_copy(identb[:], ident[:]).then_inc(consts_made, 1)
                nc.vector.tensor_copy(masks[:], masksf[:]).then_inc(consts_made, 1)
                nc.vector.tensor_tensor(coef[:, :, 0], coef[:, :, 0], bqk[:, :, 0], ALU.add).then_inc(coef_ready, 1)
                nc.vector.tensor_tensor(coef[:, :, 2], coef[:, :, 2], bqk[:, :, 1], ALU.add).then_inc(coef_ready, 1)
                dve.wait_ge(coef_ready, 2)

                link(nc.vector.memset(MX[:], 0.0))
                nc.vector.memset(ones[:], 1.0)
                nc.vector.memset(zeros[:], 0.0).then_inc(zero_made, 1)

            def layer_norm(ln, g=0, groups=1):
                tiles = range(g * NT // groups, (g + 1) * NT // groups)
                cols = slice(tiles[0], tiles[-1] + 1)
                for i in tiles:
                    last = nc.vector.bn_stats(stats[:, i, :], X[:, i, :])
                link(last)
                for i in tiles:
                    last = nc.vector.bn_aggr(mv[:, i, :], stats[:, i, :])
                link(last)
                nc.vector.tensor_scalar(rs[:, 0, cols], mv[:, cols, 1], EPS, None, ALU.add).then_inc(ln["var"], 1)
                dve.wait_ge(ln["var"], g + 1)
                dve.wait_ge(ln["sd"], g + 1)
                link(nc.vector.reciprocal(rs[:, 2, cols], rs[:, 1, cols]))
                link(nc.vector.tensor_tensor(rs[:, 3, cols], rs[:, 2, cols], rs[:, 2, cols], ALU.mult))
                link(nc.vector.tensor_tensor(rs[:, 3, cols], rs[:, 3, cols], rs[:, 0, cols], ALU.mult))
                link(nc.vector.tensor_scalar(rs[:, 3, cols], rs[:, 3, cols], -0.5, 1.5, ALU.mult, ALU.add))
                link(nc.vector.tensor_tensor(rs[:, 1, cols], rs[:, 2, cols], rs[:, 3, cols], ALU.mult))
                for i in tiles:
                    nc.vector.tensor_scalar(XN[:, i, :], X[:, i, :], mv[:, i, 0:1], rs[:, 1, i:i + 1], ALU.subtract, ALU.mult).then_inc(ln["xn"], 1)

            for g in range(4):
                dve.wait_ge(x_in[g], 16)
                layer_norm(LN[0], g, 4)
            constants()
            def pick(n, par, g):
                src = coef[:, g, :] if isinstance(g, int) else coef[:, bass.ds(g, 1), :].rearrange("p a b -> p (a b)")
                nc.vector.tensor_copy(cg[:, par, :], src).then_inc(a0["cg"], 1)
                dve.wait_ge(a0["cg"], n + 1)

            def with_positions(n, i, par, kind, at):
                side, c = i // 2, i % 2
                dve.wait_ge(a0["x_ready"], x_index(at, f"P{i}", kind) + 1)
                col = cg[:, par, 2 * side + 1:2 * side + 2]
                if i >= 2:
                    dve.wait_ge(a0["split"], 4 * n + i - 1)
                nc.vector.scalar_tensor_tensor(tq[:, i % 2, :], pos[:, c * QC:(c + 1) * QC], col, psX, ALU.mult, ALU.add).then_inc(a0["x_used"], 1)

            def low_part(n, i, par):
                side, c = i // 2, i % 2
                col = cg[:, par, 2 * side:2 * side + 1]
                dve.wait_ge(a0["hi_ready"], 4 * n + i + 1)
                nc.vector.scalar_tensor_tensor(QKs[:, 2 * side + 1, c * QC:(c + 1) * QC], tq[:, i % 2, :], col,
                                               QKs[:, 2 * side, c * QC:(c + 1) * QC].bitcast(F32), ALU.add, ALU.subtract).then_inc(a0["split"], 1)

            def row_max(n, par, i):
                h, u = i // NB, i % NB
                dve.wait_ge(a0["max_scored"], MAXES * n + i + 1)
                nc.vector.reduce_max(MXP[:, h, 4 * u:4 * u + 4], PS[:, 4 + i % 2, :].rearrange("p (b k) -> p b k", k=P), AXX).then_inc(a0["max_taken"], 1)
                if i == MAXES - 1:
                    dve.wait_ge(a0["max_taken"], MAXES * n + MAXES)
                    for qt in range(TB):
                        at = PARTIAL_AT[qt]
                        last = nc.vector.reduce_max(MX[:, par, qt:32:8], MXP[:, :, at:at + qt + 1], AXX)
                    last.then_inc(a0["maxed"], 1)

            def negate(n, kind, at):
                dve.wait_ge(a0["x_ready"], x_index(at, "T", kind) + 1)
                nc.vector.tensor_scalar(mneg[:], psX[0:32, 0:P], -1.0, None, ALU.mult).then_inc(a0["x_used"], 1)
                dve.wait_ge(a0["x_used"], x_index(at, "T", kind) + 1)
                nc.vector.tensor_copy(mh[:, 0, :], mneg[:]).then_inc(a0["neg_hi"], 1)
                dve.wait_ge(a0["neg_hi"], n + 1)
                nc.vector.tensor_tensor(mh[:, 1, :], mneg[:], mh[:, 0, :].bitcast(F32), ALU.subtract).then_inc(a0["neg"], 1)

            def reciprocals(n, kind, use):
                dve.wait_ge(a0["x_ready"], x_index(n, use, kind) + 1)
                nc.vector.reciprocal(rc[:], psX[:, 0:16]).then_inc(a0["x_used"], 1)
                dve.wait_ge(a0["x_used"], x_index(n, use, kind) + 1)
                nc.vector.tensor_copy(rb[:], rc[:, :, None].to_broadcast([P, 16, 32])).then_inc(a0["recip"], 1)

            def normalise(n, kind, use):
                dve.wait_ge(a0["x_ready"], x_index(n, use, kind) + 1)
                nc.vector.tensor_tensor(oN[:], oT[:], psX, ALU.mult).then_inc(a0["x_used"], 1)

            def add_out(n, kind, use, b, qc):
                half = use[-1] == "b"
                t0 = b * TB + qc * 4 + 2 * half
                dve.wait_ge(a0["x_ready"], x_index(n, use, kind) + 1)
                nc.vector.tensor_tensor(X[:, t0:t0 + 2, :], X[:, t0:t0 + 2, :], psX.rearrange("p (t n) -> p t n", t=2), ALU.add).then_inc(a0["x_used"], 1)

            def step(n, b, g1, kind):
                if kind != 7:
                    pick(n + 1, 1 - b, g1)
                for s in range(-1, 24):
                    use = X_AT.get(s)
                    if use in ORDERS[kind]:
                        if use[0] == "P":
                            with_positions(n + 1, int(use[1]), 1 - b, kind, n)
                            if use != "P0":
                                low_part(n + 1, int(use[1]) - 1, 1 - b)
                        elif use[0] == "S":
                            reciprocals(n, kind, use)
                        elif use[0] == "B":
                            normalise(n, kind, use)
                        else:
                            qc = int(use[1])
                            add_out(n, kind, use, (1 - b) if qc == 1 else b, qc)
                    if kind != 7:
                        if s == 4:
                            low_part(n + 1, 3, 1 - b)
                        for i in MAX_AT[s] if s >= 0 else ():
                            row_max(n + 1, 1 - b, i)
                if kind != 7:
                    negate(n + 1, kind, n)

            pick(0, 0, 0)
            for i in range(4):
                with_positions(0, i, 0, "front", 0)
                low_part(0, i, 0)
            for i in range(NT // 2):
                dve.wait_ge(v_ready, i + 1)
                if i == 0:
                    dve.wait_ge(w_in, 64)
                nc.vector.tensor_tensor(V[:, 2 * i:2 * i + 2, :], PS[:, 4 + i % 2, :].rearrange("p (t n) -> p t n", t=2),
                                        bvb[:, None, :].to_broadcast([P, 2, D]), ALU.add).then_inc(v_taken, 1)
            for i in range(MAXES):
                row_max(0, 0, i)
            negate(0, "front", 0)
            dve.wait_ge(bo_added, 1)
            step(0, 0, 0, 0)
            with dve.Fori(0, 3) as k:
                g = dve.snap(k + 1)
                step(2 * k + 1, 1, g, 1)
                step(2 * k + 2, 0, g, 1)
            step(7, 1, 0, 7)
            for use in PREV:
                if use == "S1":
                    reciprocals(8, "end", use)
                elif use == "B1":
                    normalise(8, "end", use)
                else:
                    add_out(8, "end", use, 1, 1)

            def experts(m, n, next_norm=None):
                def bc(a):
                    return a[:, :, None].to_broadcast([P, NT, 16])

                rev = small[:, None, 0:16].to_broadcast([P, NT, 16])
                tt, ts = nc.vector.tensor_tensor, nc.vector.tensor_scalar
                def hidden(q, b):
                    dve.wait_ge(m["sg"], q + 1)
                    if not isinstance(q, int) or q >= 2:
                        dve.wait_ge(m["ht"], q - 1)
                    tt(hb[:, b, :], sg[:, b, :], PS[:, b, HID:2 * HID], ALU.mult).then_inc(m["h"], 1)

                def shared_out(q):
                    i = (q if q < NSH else q - NTILE) // 2
                    dve.wait_ge(m["d"], q + 1)
                    if q % 2:
                        dve.wait_ge(m["y"], q)
                    tt(X[:, i, :], X[:, i, :], PS[:, 6 + q % 2, 0:D], ALU.add).then_inc(m["y"], 1)

                def shared(q):
                    hidden(q, q % 2)
                    if q >= 2:
                        shared_out(q - 2)

                logits = PS[:, 4, 0:256].rearrange("p (t e) -> p t e", e=16)
                dve.wait_ge(m["logits"], KC * NT)
                link(nc.vector.reduce_max(rt[:, 0], logits, AXX))
                tt(R[:, 0], logits, bc(rt[:, 0]), ALU.subtract).then_inc(m["shifted"], 1)
                dve.wait_ge(m["exps"], 1)
                link(nc.vector.reduce_sum(rt[:, 1], R[:, 1], AXX))
                link(nc.vector.reciprocal(rt[:, 1], rt[:, 1]))
                link(tt(R[:, 2], R[:, 1], bc(rt[:, 1]), ALU.mult))
                shared(0)
                src = R[:, 2]
                for j in range(2):
                    link(nc.vector.reduce_max(rt[:, 2 + j], src, AXX))
                    link(tt(R[:, 3], src, bc(rt[:, 2 + j]), ALU.is_equal))
                    link(tt(R[:, 3], R[:, 3], rev, ALU.mult))
                    shared(2 * j + 1)
                    link(nc.vector.reduce_max(rt[:, 4 + j], R[:, 3], AXX))
                    link(tt(R[:, 4 + j], rev, bc(rt[:, 4 + j]), ALU.is_equal))
                    if j == 0:
                        link(nc.vector.scalar_tensor_tensor(R[:, 6], R[:, 4], -2.0, R[:, 2], ALU.mult, ALU.add))
                        src = R[:, 6]
                        shared(2)
                tt(R[:, 7], R[:, 4], R[:, 5], ALU.add).then_inc(m["onehot"], 1)
                shared(4)
                shared(COUNT_AT)
                nc.vector.memset(carry[:, 0, :], 0.0)
                dve.wait_ge(m["counted"], 1)
                totals = PS[:, 3, 256:512].rearrange("p (t e) -> p t e", e=16)
                ranks = PS[:, 3, 0:256].rearrange("p (t e) -> p t e", e=16)
                link(nc.vector.tensor_copy(carry[:, 1, :], totals[:, 0, :]))
                for i in range(1, NT):
                    link(tt(carry[:, i + 1, :], carry[:, i, :], totals[:, i, :], ALU.add))
                    if i % 7 == 0:
                        shared(COUNT_AT + i // 7)
                link(ts(tl[:, 0], carry[:, NT, :], 1.0 / P, 127.0 / 128 - 127.0 / 256, ALU.mult, ALU.add))
                link(nc.vector.tensor_copy(tli[:], tl[:, 0]))
                link(nc.vector.tensor_copy(tl[:, 0], tli[:]))
                shared(COUNT_AT + 3)
                link(tt(lt[:], small[:, 16:272].rearrange("p (a b) -> p a b", b=16), tl[:, 0, None, :].to_broadcast([P, 16, 16]), ALU.mult))
                link(nc.vector.reduce_sum(tl[:, 1], lt[:], AXX))
                link(tt(tl[:, 2], tl[:, 1], tl[:, 0], ALU.add))
                link(ts(tl[:, 3], tl[:, 1], float(P), None, ALU.mult))
                shared(COUNT_AT + 4)
                link(tt(R[:, 3], carry[:, 0:NT, :], ranks, ALU.add))
                link(tt(R[:, 3], R[:, 3], tl[:, 3, None, :].to_broadcast([P, NT, 16]), ALU.add))
                for j in range(2):
                    link(tt(R[:, 6], R[:, 3], R[:, 4 + j], ALU.mult))
                    link(nc.vector.reduce_sum(rt[:, 6 + j], R[:, 6], AXX))
                    nc.vector.tensor_copy(slot[:, j, :], rt[:, 6 + j]).then_inc(m["slot"], 1)
                    shared(COUNT_AT + 5 + j)
                link(tt(owner[:], tl[:, 2, None, :].to_broadcast([P, NTILE, 16]), small[:, 272:].rearrange("p (g e) -> p g e", e=16), ALU.is_le))
                link(nc.vector.reduce_sum(eidf[:], owner[:], AXX))
                shared(COUNT_AT + 7)
                link(ts(eidf[:], eidf[:], 15.0, None, ALU.min))
                nc.vector.tensor_copy(eid[:], eidf[:]).then_inc(m["eid"], 1)

                def tile_out(q, b):
                    dve.wait_ge(m["d"], q + 1)
                    if not isinstance(q, int) or q >= NSH + 2:
                        dve.wait_ge(m[f"stored{b}"], 16 * ((q - NSH) // 2) if isinstance(q, int) else stored)
                    nc.vector.tensor_copy(ys[:, b, :], PS[:, 6 + b, 0:D]).then_inc(m["y"], 1)

                for q in range(COUNT_AT + 8, NSH):
                    shared(q)
                for q in range(NSH, NSH + 4):
                    hidden(q, q % 2)
                    if q < NSH + 2:
                        shared_out(q - 2)
                    else:
                        tile_out(q - 2, q % 2)
                with dve.Fori(0, NTILE // 2 - 2) as k:
                    for j in range(2):
                        q = NSH + 4 + 2 * k + j
                        hidden(q, j)
                        stored = 16 * k + 16
                        tile_out(q - 2, j)
                for q in range(NSH + NTILE, NSH + NTILE + 2):
                    hidden(q, q % 2)
                    tile_out(q - 2, q % 2)
                for i in range(NT):
                    for q in range(NSH + NTILE + 2 + 2 * i, NSH + NTILE + 4 + 2 * i):
                        if q < STEPS:
                            hidden(q, q % 2)
                        if q < STEPS + 2:
                            shared_out(q - 2)
                    if i == NTAIL // 2:
                        dve.wait_ge(m["y"], STEPS)
                    dve.wait_ge(m[f"got{i % 4}"], 32 * (i // 4 + 1))
                    for j in range(2):
                        if j:
                            dve.wait_ge(m["added"], 2 * i + 1)
                        nc.vector.scalar_tensor_tensor(X[:, i, :], yg[:, i % 4, j, :], rt[:, 2 + j, i:i + 1], X[:, i, :], ALU.mult, ALU.add).then_inc(m["added"], 1)
                    if next_norm and i % 4 == 3:
                        dve.wait_ge(m["added"], 2 * i + 2)
                        layer_norm(next_norm, i // 4, 4)

            dve.wait_ge(a0["x_used"], x_index(8, "W1b", "end") + 1)
            for g in range(2):
                layer_norm(LN[1], g, 2)
            experts(moe[0], 0, LN[2])

            def attention1():
                dve.wait_ge(a1["wt_in"], 64)
                nc.vector.tensor_copy(selb[:], self_[:]).then_inc(a1["sel"], 1)
                link(nc.vector.memset(MX1[:], 0.0))
                dve.wait_ge(a1["made"], 3)

                def rotate(n, use, kind, at):
                    i = CHUNKS.index(use)
                    c, j = 10 * n + i, i % 2
                    cols = slice(int(use[-1]) * QC, int(use[-1]) * QC + QC)
                    bank = x1_bank(use, kind)
                    dve.wait_ge(a1["x_ready"], x1_index(at, use, kind) + 1)
                    if not (isinstance(c, int) and c < 2):
                        dve.wait_ge(a1["summed"], c - 1)
                    nc.vector.tensor_tensor(r2[64:96, j, :], bank[96:128, :], rope[96:128, 1, cols], ALU.mult)
                    nc.vector.tensor_tensor(r2[96:128, j, :], bank[64:96, :], rope[64:96, 1, cols], ALU.mult)
                    nc.vector.tensor_tensor(r1[64:128, j, :], bank[64:128, :], rope[64:128, 0, cols], ALU.mult).then_inc(a1["roped"], 1)
                    dve.wait_ge(a1["plain"], c + 1)
                    dve.wait_ge(a1["roped"], c + 1)
                    nc.vector.tensor_copy(rt1[:], ones[:, 0:1]).then_inc(a1["x_used"], 1)

                def row_max(n, par, i):
                    h, u = i // NB, i % NB
                    dve.wait_ge(a1["max_scored"], MAXES * n + i + 1)
                    nc.vector.reduce_max(MXP1[:, h, 4 * u:4 * u + 4], PS[:, 4 + i % 2, :].rearrange("p (b k) -> p b k", k=P), AXX).then_inc(a1["max_taken"], 1)
                    if i == MAXES - 1:
                        dve.wait_ge(a1["max_taken"], MAXES * n + MAXES)
                        for qt in range(TB):
                            at = PARTIAL_AT[qt]
                            last = nc.vector.reduce_max(MX1[:, par, qt:32:8], MXP1[:, :, at:at + qt + 1], AXX)
                        last.then_inc(a1["maxed"], 1)

                def negate(n, kind, at):
                    i = x1_index(at, "T", kind)
                    dve.wait_ge(a1["x_ready"], i + 1)
                    nc.vector.tensor_scalar(mn1[:, 0, :], psX[0:32, 0:P], -1.0, None, ALU.mult).then_inc(a1["x_used"], 1)
                    dve.wait_ge(a1["x_used"], i + 1)
                    nc.vector.tensor_copy(mb1[:, 0, :], mn1[:, 0, :]).then_inc(a1["neg_mid"], 1)
                    dve.wait_ge(a1["neg_mid"], 2 * n + 1)
                    nc.vector.tensor_tensor(mn1[:, 1, :], mn1[:, 0, :], mb1[:, 0, :], ALU.subtract).then_inc(a1["neg_mid"], 1)
                    dve.wait_ge(a1["neg_mid"], 2 * n + 2)
                    nc.vector.tensor_copy(mb1[:, 1, :], mn1[:, 1, :]).then_inc(a1["neg"], 1)

                def other(n, use, kind, b):
                    i = x1_index(n, use, kind)
                    dve.wait_ge(a1["x_ready"], i + 1)
                    if use == "A":
                        nc.vector.tensor_copy(WQ[:, :, :, 0:64].rearrange("p h k c -> p (h k) c"), psX.rearrange("p (a c) -> p a c", c=64)).then_inc(a1["x_used"], 1)
                    elif use == "V":
                        nc.vector.tensor_copy(WVO[:].rearrange("p a n -> p (a n)"), psX).then_inc(a1["x_used"], 1)
                    else:
                        t0 = (1 - b) * TB + 2 * int(use[1])
                        nc.vector.tensor_tensor(X[:, t0:t0 + 2, :], X[:, t0:t0 + 2, :], psX.rearrange("p (t n) -> p t n", t=2), ALU.add).then_inc(a1["x_used"], 1)

                def finish(n, c):
                    h, qc, i = c // 2, c % 2, 8 * n + c
                    out = PS[:, 3 if qc == 0 else 6, 0:260].rearrange("p (t e) -> p t e", e=65)
                    dve.wait_ge(a1["pv"], 48 * n + 12 * h + (4 if qc == 0 else 12))
                    if not (isinstance(n, int) and n == 0 and c < 2):
                        dve.wait_ge(a1["evac"], i - 1)
                    nc.vector.reciprocal(rc1[:, qc, :], out[:, :, 64]).then_inc(a1["recip"], 1)
                    dve.wait_ge(a1["recip"], i + 1)
                    nc.vector.tensor_tensor(oq1[:, h // 2, 4 * qc:4 * qc + 4, h % 2, :], out[:, :, 0:64],
                                            rc1[:, qc, :, None].to_broadcast([P, 4, 64]), ALU.mult).then_inc(a1["evac"], 1)

                def step(n, b, kind):
                    for s in range(-1, 48):
                        if s == 2 and kind != 0:
                            finish(n - 1, 7)
                        for h in range(4):
                            if s == 12 * h + 6:
                                finish(n, 2 * h)
                            if s == 12 * h + 14:
                                finish(n, 2 * h + 1)
                        for use in X1_AT[s]:
                            if has1(use, kind) and use[0] != "N":
                                if use in CHUNKS:
                                    rotate(n + 1, use, kind, n)
                                else:
                                    other(n, use, kind, b)
                        if kind != 7 and s >= 0:
                            for i in MAX1_AT[s]:
                                row_max(n + 1, 1 - b, i)
                    if kind != 7:
                        negate(n + 1, kind, n)

                other(0, "A", "front", 0)
                for use in CHUNKS:
                    rotate(0, use, "front", 0)
                    for i in FRONT_MAX.get(use, ()):
                        row_max(0, 0, i)
                for i in range(3 * NB, MAXES):
                    row_max(0, 0, i)
                negate(0, "front", 0)
                step(0, 0, 0)
                with dve.Fori(0, 3) as k:
                    step(2 * k + 1, 1, "odd")
                    step(2 * k + 2, 0, "even")
                step(7, 1, 7)
                finish(7, 7)
                for use in PREV1[1:]:
                    other(8, use, "end", 0)

            dve.wait_ge(moe[0]["added"], 2 * NT)
            attention1()
            dve.wait_ge(a1["x_used"], x1_index(8, "O3", "end") + 1)
            for g in range(2):
                layer_norm(LN[3], g, 2)
            experts(moe[1], 1)

        @block.tensor
        def _(pe):

            def layer_norm(ln, behind=None, lag=2):
                for i in range(NT // 2):
                    if behind and i >= lag:
                        behind(i - lag)
                    pe.wait_ge(ln["xn"], 2 * i + 2)
                    if i >= 4:
                        pe.wait_ge(ln["xt"], i - 3)
                    for c in range(KC):
                        for t in range(2):
                            last = nc.tensor.transpose(PS[:, i % 4, (2 * c + t) * P:(2 * c + t + 1) * P], XN[:, 2 * i + t, c * P:(c + 1) * P], ident[:])
                    last.then_inc(ln["t"], 1)

            pe.wait_ge(ident_in, 16)
            layer_norm(LN[0])
            def free_x(n, use, kind):
                i = x_index(n, use, kind)
                if not (isinstance(i, int) and i == 0):
                    pe.wait_ge(a0["x_used"], i)

            def max_scores(n, par, i, k_round):
                if i % NB == 0:
                    pe.wait_ge(copied[par][i // NB], k_round)
                if not (isinstance(n, int) and n == 0 and i < 2):
                    pe.wait_ge(a0["max_taken"], MAXES * n + i - 1)
                h, at = i // NB, 0
                for qt, k0, blocks in BANKS[i % NB]:
                    diag = k0 + blocks == qt + 1
                    out = PS[:, 4 + i % 2, at * P:(at + blocks) * P]
                    last = nc.tensor.matmul(out, QS[:, par, h, qt * P:(qt + 1) * P], KS[:, par, h, k0 * P:(k0 + blocks) * P], start=True, stop=not diag)
                    if diag:
                        last = nc.tensor.matmul(PS[:, 4 + i % 2, (at + blocks - 1) * P:(at + blocks) * P], identb[:], masks[:, 0, :], start=False, stop=True)
                    at += blocks
                last.then_inc(a0["max_scored"], 1)

            def turn(n, par, at, kind):
                free_x(at, "T", kind)
                pe.wait_ge(a0["maxed"], n + 1)
                nc.tensor.transpose(psX[:, 0:P], MX[:, par, :], ident[:]).then_inc(a0["x_ready"], 1)

            def scores(n, par, s):
                qc, kt, pair = SLOTS[s]
                lo = first_query(qc, kt)
                diag = kt * P >= qc * QC
                if not (isinstance(n, int) and n == 0 and s < 2):
                    pe.wait_ge(a0["probs"], 24 * n + s - 1)
                for j in range(2):
                    h, bank = 2 * pair + j, 2 * (s % 2) + j
                    last = nc.tensor.matmul(PS[:, bank, wide(lo):QC], KS[:, par, h, kt * P:(kt + 1) * P], QS[:, par, h, qc * QC + wide(lo):(qc + 1) * QC],
                                            start=True, stop=not diag)
                    if diag:
                        last = nc.tensor.matmul(PS[:, bank, lo:lo + P], identb[:], masks[:, 1, :], start=False, stop=True)
                last.then_inc(a0["scores"], 1)

            def values(n, b, s):
                qc, kt, pair = SLOTS[s]
                lo = first_query(qc, kt)
                pe.wait_ge(a0["probs"], 24 * n + s + 1)
                if pair == 0 and kt == 0:
                    if not (isinstance(n, int) and n == 0 and qc == 0):
                        pe.wait_ge(a0["evac"], 2 * n + qc)
                    pe.wait_ge(a0["staged"], n + 1)
                for j in range(2):
                    h = 2 * pair + j
                    last = nc.tensor.matmul(psO[32 * h:32 * h + 32, lo:QC], VS[:, b, kt, h, :], PT[:, s % 3, j, lo:QC],
                                            start=(kt == 0), stop=(kt == (3 if qc == 0 else 7)), skip_group_check=True)
                last.then_inc(a0["pv"], 1)

            def sums(n, use, kind):
                free_x(n, use, kind)
                pe.wait_ge(a0["evac"], 2 * n + (1 if use[1] == "0" else 0))
                for t in range(4):
                    last = nc.tensor.matmul(psX[:, 4 * t:4 * t + 4], oT[:, t * P:(t + 1) * P], spread[:, 0:P:32], start=True, stop=True)
                last.then_inc(a0["x_ready"], 1)

            def spread_out(n, use, kind):
                pe.wait_ge(a0["recip"], 2 * n + (1 if use[1] == "0" else 0))
                for t in range(4):
                    last = nc.tensor.matmul(psX[:, t * P:(t + 1) * P], rb[:, 4 * t:4 * t + 4, :].rearrange("p a b -> p (a b)"), ident[:], start=True, stop=True)
                last.then_inc(a0["x_ready"], 1)

            def out_rows(n, use, kind, g):
                half, qc = use[-1] == "b", int(use[1])
                free_x(n, use, kind)
                for t in range(2):
                    w = wo0[:, g, :] if isinstance(g, int) else wo0[:, bass.ds(g, 1), :].rearrange("p a n -> p (a n)")
                    last = nc.tensor.matmul(psX[:, t * D:(t + 1) * D], oN[:, (2 * half + t) * P:(2 * half + t + 1) * P], w, start=True, stop=True)
                last.then_inc(a0["x_ready"], 1)

            def step(n, b, g, gprev, kind, k_here, k_next, w_need=None):
                for s in range(-1, 24):
                    if s == 0:
                        pe.wait_ge(a0[f"row{b}"], k_here)
                    if s >= 0:
                        scores(n, b, s)
                    if s >= 2:
                        values(n, b, s - 2)
                    use = X_AT.get(s)
                    if use in ORDERS[kind]:
                        if use[0] == "P":
                            if use == "P0" and w_need is not None:
                                pe.wait_ge(a0["w_in"], w_need)
                            i = int(use[1])
                            side, c = i // 2, i % 2
                            free_x(n, use, kind)
                            for kc in range(KC):
                                last = nc.tensor.matmul(psX, wqk[:, 2 * side + kc, :], XT[:, kc, (1 - b) * SEQ + c * QC:(1 - b) * SEQ + (c + 1) * QC],
                                                        start=(kc == 0), stop=(kc == 1))
                            last.then_inc(a0["x_ready"], 1)
                        elif use[0] == "S":
                            sums(n, use, kind)
                        elif use[0] == "B":
                            spread_out(n, use, kind)
                        else:
                            out_rows(n, use, kind, gprev if use[1] == "1" else g)
                    if kind != 7:
                        for i in MAX_AT[s] if s >= 0 else ():
                            max_scores(n + 1, 1 - b, i, k_next)
                values(n, b, 22)
                values(n, b, 23)
                if kind != 7:
                    turn(n + 1, 1 - b, n, kind)

            pe.wait_ge(a0["w_in"], 16)
            for i in range(4):
                side, c = i // 2, i % 2
                pe.wait_ge(LN[0]["xt"], 2 * c + 2)
                free_x(0, f"P{i}", "front")
                for kc in range(KC):
                    last = nc.tensor.matmul(psX, wqk[:, 2 * side + kc, :], XT[:, kc, c * QC:(c + 1) * QC], start=(kc == 0), stop=(kc == 1))
                last.then_inc(a0["x_ready"], 1)
            pe.wait_ge(w_in, 64)
            for i in range(NT // 2):
                pe.wait_ge(LN[0]["xt"], i + 1)
                if i >= 2:
                    pe.wait_ge(v_taken, i - 1)
                for t in range(2):
                    for c in range(KC):
                        last = nc.tensor.matmul(PS[:, 4 + i % 2, t * D:(t + 1) * D], XT[:, c, (2 * i + t) * P:(2 * i + t + 1) * P], wv[:, c, :],
                                                start=(c == 0), stop=(c == KC - 1))
                last.then_inc(v_ready, 1)
            pe.wait_ge(v_taken, NT // 2)
            pe.wait_ge(consts_made, 2)
            for i in range(MAXES):
                max_scores(0, 0, i, 128)
            turn(0, 0, 0, "front")
            step(0, 0, 0, 0, 0, 32, 128)
            with pe.Fori(0, 3) as k:
                g1 = pe.snap(k + 1)
                step(2 * k + 1, 1, k, k, 1, 32 * k + 32, 128 * k + 256, 16 * k + 32)
                step(2 * k + 2, 0, g1, k, 1, 32 * k + 64, 128 * k + 256)
            step(7, 1, 3, 3, 7, 128, 0)
            for use in PREV:
                if use == "S1":
                    sums(8, use, "end")
                elif use == "B1":
                    spread_out(8, use, "end")
                else:
                    out_rows(8, use, "end", 3)

            def experts(m, ln):
                pe.wait_ge(m["gate_in"], 16)

                def logits(pair):
                    pe.wait_ge(ln["xt"], pair + 1)
                    for i in (2 * pair, 2 * pair + 1):
                        for kc in range(KC):
                            nc.tensor.matmul(PS[:, 4, i * 16:i * 16 + 16], XT[:, kc, i * P:(i + 1) * P], gw[:, kc, :],
                                             start=(kc == 0), stop=(kc == 1)).then_inc(m["logits"], 1)

                layer_norm(ln, logits)
                logits(NT // 2 - 2)
                logits(NT // 2 - 1)
                pe.wait_ge(m["shared_in"], 16 * 3)

                def count():
                    pe.wait_ge(m["onehot"], 1)
                    hot = R[:, 7].rearrange("p t e -> p (t e)")
                    nc.tensor.matmul(PS[:, 3, 0:256], before[:], hot, start=True, stop=True)
                    nc.tensor.matmul(PS[:, 3, 256:512], ones[:], hot, start=True, stop=True).then_inc(m["counted"], 1)

                def up(q, b, g):
                    e = None if g is None else expert(g)
                    if not (isinstance(q, int) and q < 2):
                        pe.wait_ge(m["h"], q - 1)
                    if g is None:
                        i = (q if q < NSH else q - NTILE) // 2
                        x = [XT[:, kc, i * P:(i + 1) * P] for kc in range(KC)]
                        w = [W13[:, kc, 16 + q % 2, :] for kc in range(KC)]
                    else:
                        pe.wait_ge(m["xT"], g + 1)
                        x = [xTs[:, b, kc, :] for kc in range(KC)]
                        w = [W13[:, kc, bass.ds(e, 1), :].rearrange("p a n -> p (a n)") for kc in range(KC)]
                    for kc in range(KC):
                        last = nc.tensor.matmul(PS[:, b, 0:2 * HID], x[kc], w[kc], start=(kc == 0), stop=(kc == 1))
                    last.then_inc(m["u"], 1)

                def expert(g):
                    at = eid[0:1, g:g + 1] if isinstance(g, int) else eid[0:1, bass.ds(g, 1)]
                    return pe.value_load(at, min_val=0, max_val=15)

                def turn_x(g, b, round4):
                    j = g % 4 if isinstance(g, int) else round4[0]
                    pe.wait_ge(m[f"xs{j}"], 16 * (g // 4 + 1) if isinstance(g, int) else round4[1])
                    if not (isinstance(g, int) and g < 2):
                        pe.wait_ge(m["xT"], g - 1)
                    for kc in range(KC):
                        last = nc.tensor.transpose(PS[:, 2 + b, kc * P:(kc + 1) * P], xs[:, j, kc * P:(kc + 1) * P], ident[:])
                    last.then_inc(m["t"], 1)

                def turn_h(q, b):
                    pe.wait_ge(m["h"], q + 1)
                    if not (isinstance(q, int) and q < 2):
                        pe.wait_ge(m["hT"], q - 1)
                    for half in range(2):
                        last = nc.tensor.transpose(PS[0:HH, 4 + b, half * P:(half + 1) * P], hb[:, b, half * HH:(half + 1) * HH], ident[:])
                    last.then_inc(m["ht"], 1)

                def down(q, b, g):
                    e = None if g is None else expert(g)
                    pe.wait_ge(m["hT"], q + 1)
                    if not (isinstance(q, int) and q < 2):
                        pe.wait_ge(m["y"], q - 1)
                    if g is None:
                        w = [W2[:, half, 16 + q % 2, :] for half in range(2)]
                    else:
                        w = [W2[:, half, bass.ds(e, 1), :].rearrange("p a n -> p (a n)") for half in range(2)]
                    for half in range(2):
                        last = nc.tensor.matmul(PS[:, 6 + b, 0:D], hT[:, b, half, :], w[half], start=(half == 0), stop=(half == 1))
                    last.then_inc(m["d"], 1)

                for q in range(NSH):
                    up(q, q % 2, None)
                    if q == NSH - 1:
                        pe.wait_ge(m["eid"], 1)
                        pe.wait_ge(m["w_in"], 16 * 3)
                        turn_x(0, 0, None)
                    if q >= 1:
                        turn_h(q - 1, 1 - q % 2)
                    if q >= 2:
                        down(q - 2, q % 2, None)
                    if q == COUNT_AT:
                        count()

                def step(g, b, turn, lag):
                    up(NSH + g, b, g)
                    if turn is not None:
                        turn_x(turn, 1 - b, lag)
                    turn_h(NSH + g - 1, 1 - b)
                    if isinstance(g, int) and g < 2:
                        down(NSH + g - 2, b, None)
                    else:
                        down(NSH + g - 2, b, g - 2)

                for g in range(4):
                    step(g, g % 2, g + 1, None)
                with pe.Fori(0, NTILE // 4 - 2) as k:
                    for j in range(4):
                        step(4 * k + 4 + j, j % 2, 4 * k + 5 + j, ((j + 1) % 4, 16 * k + 32 + (16 if j == 3 else 0)))
                for g in range(NTILE - 4, NTILE):
                    step(g, g % 2, g + 1 if g + 1 < NTILE else None, None)
                for q in range(NSH + NTILE, STEPS):
                    up(q, q % 2, None)
                    turn_h(q - 1, 1 - q % 2)
                    down(q - 2, q % 2, q - 2 - NSH if q - 2 < NSH + NTILE else None)
                turn_h(STEPS - 1, 1)
                down(STEPS - 2, 0, None)
                down(STEPS - 1, 1, None)

            def attention1():
                def latent(pair):
                    if pair % 2 == 0:
                        return
                    i = pair // 2
                    pe.wait_ge(a1["wt_in"], 64)
                    pe.wait_ge(LN[2]["xt"], pair + 1)
                    if i >= 2:
                        pe.wait_ge(a1["cT"], i - 1)
                    for kc in range(KC):
                        last = nc.tensor.matmul(PS[0:64, 4 + i % 2, :], wc[:, kc, :], XT[:, kc, i * QC:(i + 1) * QC], start=(kc == 0), stop=(kc == 1))
                    last.then_inc(a1["c_ready"], 1)

                layer_norm(LN[2], latent, 1)
                latent(NT // 2 - 1)
                def free_x(i):
                    if not (isinstance(i, int) and i == 0):
                        pe.wait_ge(a1["x_used"], i)

                def chunk(n, b, use, kind, at):
                    i, bank = x1_index(at, use, kind), x1_bank(use, kind)
                    free_x(i - 1 if kind == "front" else i)
                    lo = b * SEQ + int(use[-1]) * QC
                    if use[0] == "K":
                        last = nc.tensor.matmul(bank, WK[:], cT[:, lo:lo + QC], start=True, stop=True)
                    else:
                        for kc in range(KC):
                            last = nc.tensor.matmul(bank, WQ[:, int(use[1]), kc, :], XT[:, kc, lo:lo + QC], start=(kc == 0), stop=(kc == 1))
                    last.then_inc(a1["x_ready"], 1)

                def other(n, use, kind):
                    free_x(x1_index(n, use, kind))
                    if use == "A":
                        for h in range(4):
                            for kc in range(KC):
                                at = (h * KC + kc) * 64
                                last = nc.tensor.matmul(psX[:, at:at + 64], wqn[:, h, kc * P:(kc + 1) * P], wkT[:], start=True, stop=True)
                    elif use == "V":
                        for h in range(4):
                            last = nc.tensor.matmul(psX[64 * (h % 2):64 * (h % 2) + 64, (h // 2) * D:(h // 2 + 1) * D], wvT[:], wog[:, h, :], start=True, stop=True)
                    elif use[0] == "N":
                        pair, qc = int(use[1]) // 2, int(use[1]) % 2
                        pe.wait_ge(a1["evac"], 8 * n + {"N0": 3, "N1": 4, "N2": 7, "N3": 0}[use])
                        for t in range(4):
                            last = nc.tensor.transpose(psX[:, t * P:(t + 1) * P], oq1[:, pair, 4 * qc + t].rearrange("p h c -> p (h c)"), ident[:])
                    else:
                        for t in range(2):
                            tok = (2 * int(use[1]) + t) * P
                            for pair in range(2):
                                last = nc.tensor.matmul(psX[:, t * D:(t + 1) * D], oN1[:, pair, tok:tok + P], WVO[:, pair, :], start=(pair == 0), stop=(pair == 1))
                    last.then_inc(a1["x_ready"], 1)

                def max_scores(n, par, i):
                    if i % NB == 0:
                        pe.wait_ge(a1["hi_ready"], 10 * n + 4 + 2 * (i // NB))
                    if not (isinstance(n, int) and n == 0 and i < 2):
                        pe.wait_ge(a1["max_taken"], MAXES * n + i - 1)
                    h, at = i // NB, 0
                    for qt, k0, blocks in BANKS[i % NB]:
                        diag = k0 + blocks == qt + 1
                        out = PS[:, 4 + i % 2, at * P:(at + blocks) * P]
                        last = nc.tensor.matmul(out, QH[:, par, h, qt * P:(qt + 1) * P], KH[:, par, k0 * P:(k0 + blocks) * P], start=True, stop=not diag)
                        if diag:
                            last = nc.tensor.matmul(PS[:, 4 + i % 2, (at + blocks - 1) * P:(at + blocks) * P], identb[:], masks[:, 0, :], start=False, stop=True)
                        at += blocks
                    last.then_inc(a1["max_scored"], 1)

                def turn(n, par, kind, at):
                    free_x(x1_index(at, "T", kind))
                    pe.wait_ge(a1["maxed"], n + 1)
                    nc.tensor.transpose(psX[:, 0:P], MX1[:, par, :], ident[:]).then_inc(a1["x_ready"], 1)

                def scores(n, par, s):
                    h, qc, kt = SLOTS1[s]
                    lo = first_query(qc, kt)
                    diag = kt * P >= qc * QC
                    if not (isinstance(n, int) and n == 0 and s < 3):
                        pe.wait_ge(a1["probs"], 48 * n + s - 2)
                    out = PS[:, s % 3, wide(lo):QC]
                    keys, queries = slice(kt * P, (kt + 1) * P), slice(qc * QC + wide(lo), (qc + 1) * QC)
                    nc.tensor.matmul(out, KH[:, par, keys], QH[:, par, h, queries], start=True, stop=False)
                    nc.tensor.matmul(out, KH[:, par, keys], QL[:, par, h, queries], start=False, stop=False)
                    nc.tensor.matmul(out, KL[:, par, keys], QH[:, par, h, queries], start=False, stop=False)
                    last = nc.tensor.matmul(PS[:, s % 3, lo:QC], selb[:, h, :], MR[:, par, qc * QC + lo:(qc + 1) * QC], start=False, stop=not diag)
                    if diag:
                        last = nc.tensor.matmul(PS[:, s % 3, lo:lo + P], identb[:], masks[:, 1, :], start=False, stop=True)
                    last.then_inc(a1["scores"], 1)

                def values(n, b, s):
                    h, qc, kt = SLOTS1[s]
                    lo = first_query(qc, kt)
                    c = 2 * h + qc
                    pe.wait_ge(a1["probs"], 48 * n + s + 1)
                    if kt == 0 and not (isinstance(n, int) and n == 0 and c < 2):
                        pe.wait_ge(a1["evac"], 8 * n + c - 1)
                    for t in range(lo // P, 4):
                        last = nc.tensor.matmul(PS[:, 3 if qc == 0 else 6, 65 * t:65 * t + 65], PT1[:, s % 4, t * P:(t + 1) * P], CA[:, b * TB + kt, :],
                                                start=(kt == 0 and t == 0), stop=(kt == 4 * qc + 3 and t == 3))
                    last.then_inc(a1["pv"], 1)

                def step(n, b, kind, rows, w_need=None):
                    for s in range(-1, 48):
                        if s == 0:
                            pe.wait_ge(a1[f"row{b}"], rows)
                            pe.wait_ge(a1["split"], 10 * n + 10)
                        if s >= 0:
                            scores(n, b, s)
                        if s >= 2:
                            values(n, b, s - 2)
                        for use in X1_AT[s]:
                            if has1(use, kind):
                                if use in CHUNKS:
                                    if use == "K0" and w_need is not None:
                                        pe.wait_ge(a1["w_in"], w_need)
                                    chunk(n + 1, 1 - b, use, kind, n)
                                else:
                                    other(n, use, kind)
                        if kind != 7 and s >= 0:
                            for i in MAX1_AT[s]:
                                max_scores(n + 1, 1 - b, i)
                    values(n, b, 46)
                    values(n, b, 47)
                    if kind != 7:
                        turn(n + 1, 1 - b, kind, n)

                pe.wait_ge(a1["w_in"], 16 * 9)
                other(0, "A", "front")
                pe.wait_ge(a1["cT"], 4)
                for use in CHUNKS:
                    chunk(0, 0, use, "front", 0)
                    if use == TURN_BEHIND:
                        for i in range(2):
                            for t in range(8):
                                last = nc.tensor.transpose(PS[:, i, t * 64:(t + 1) * 64], cT[:, (8 * i + t) * P:(8 * i + t + 1) * P], ident[0:64, 0:64])
                            last.then_inc(a1["ct_turned"], 1)
                    for i in FRONT_MAX.get(use, ()):
                        max_scores(0, 0, i)
                for i in range(3 * NB, MAXES):
                    max_scores(0, 0, i)
                turn(0, 0, "front", 0)
                pe.wait_ge(a1["CA"], 2)
                pe.wait_ge(a1["sel"], 1)
                step(0, 0, 0, 32)
                with pe.Fori(0, 3) as k:
                    step(2 * k + 1, 1, "odd", 32 * k + 32, 144 * k + 288)
                    step(2 * k + 2, 0, "even", 32 * k + 64)
                step(7, 1, 7, 128)
                for use in PREV1:
                    other(8, use, "end")

            experts(moe[0], LN[1])
            attention1()
            experts(moe[1], LN[3])


def laid_out(v):
    def heads(w, n=1):
        w = w.reshape(-1, 4, 4, 16)
        return np.pad(w, ((0, 0), (0, 0), (0, 0), (0, 16))).reshape(-1, 4, P).transpose(1, 0, 2)
    f = lambda name: np.asarray(v[name])
    wq, wk = heads(f("L0_attn_wq")), heads(f("L0_attn_wk"))
    wqk = np.stack([wq.reshape(4, KC, P, P), wk.reshape(4, KC, P, P)], 1).transpose(0, 3, 1, 2, 4).reshape(4, P, 4, P)
    out = {
        "x": f("L0_attn_x").reshape(T, D),
        "wqk": np.pad(wqk, ((0, 1), (0, 0), (0, 0), (0, 0))),
        "bqk": np.stack([heads(f("L0_attn_bq")[None])[:, 0], heads(f("L0_attn_bk")[None])[:, 0]], -1).transpose(1, 0, 2),
        "wv": f("L0_attn_wv"), "bv": f("L0_attn_bv")[None], "bo": f("L0_attn_bo")[None],
        "wo0": np.pad(f("L0_attn_wo").reshape(4, 4, 16, D), ((0, 0), (0, 0), (0, 16), (0, 0))).reshape(4, P, D),
    }
    def moe_up(l):
        w = np.concatenate([f(f"L{l}_ffn_w1"), f(f"L{l}_ffn_w3")], 1)
        a, b = f(f"L{l}_ffn_sw1").reshape(2, HID, D), f(f"L{l}_ffn_sw3").reshape(2, HID, D)
        w = np.concatenate([w, np.concatenate([a, b], 1)], 0)
        return w.reshape(NE, 2 * HID, KC, P).transpose(3, 2, 0, 1)
    def moe_down(l):
        s = f(f"L{l}_ffn_sw2").reshape(D, 2, HID).transpose(1, 0, 2)
        w = np.concatenate([f(f"L{l}_ffn_w2"), s], 0)
        return w.reshape(NE, D, 2, HH).transpose(3, 2, 0, 1)
    wqkv = f("L1_attn_Wqkv")
    q = wqkv[:, :16 * 192].reshape(D, 4, 4, 192)
    out["wqn"] = q[..., :128].transpose(1, 3, 2, 0)
    out["wqr"] = q[..., 128:].reshape(KC, P, 4, 4, 64).transpose(2, 1, 3, 0, 4)
    out["wc"] = wqkv[:, 16 * 192:].reshape(KC, P, 64).transpose(1, 0, 2)
    up = f("L1_attn_Wk_up").reshape(64, 4, 192)
    out["wkT"] = up[..., :128].transpose(1, 2, 0)
    out["wkr"] = up[..., 128:].transpose(1, 0, 2)
    out["wvT"] = f("L1_attn_Wv_up").reshape(64, 4, 128).transpose(1, 2, 0)
    out["wog"] = f("L1_attn_Wo").reshape(4, 4, 128, D).transpose(0, 2, 1, 3)
    for name in ("wqn", "wqr", "wkT", "wkr", "wvT", "wog"):
        out[name] = np.pad(out[name], ((0, 1),) + ((0, 0),) * (out[name].ndim - 1))
    out["w13"] = np.stack([moe_up(0), moe_up(1)])
    out["w2"] = np.stack([moe_down(0), moe_down(1)])
    out["gw"] = np.stack([f(f"L{l}_ffn_gate_w").reshape(16, KC, P).transpose(2, 1, 0) for l in range(2)])
    out.update(tables())
    return {k: np.ascontiguousarray(a) for k, a in out.items()}


def kernel(**inputs):
    import concourse.bacc as bacc
    from concourse.bass_utils import run_bass_kernel_spmd

    nc = bacc.Bacc("TRN2", target_bir_lowering=False, num_devices=1)
    arrays, args = {}, {}
    for name, a in laid_out(inputs).items():
        arrays[f"in_{name}_dram"] = a
        args[name] = nc.dram_tensor(f"in_{name}_dram", a.shape, mybir.dt.from_np(a.dtype), kind="ExternalInput").ap()
    args["out"] = nc.dram_tensor("out_dram", (T, D), F32, kind="ExternalOutput").ap()
    build(nc, **args)
    r = run_bass_kernel_spmd(nc, [arrays], core_ids=[0])
    return r.results[0]["out_dram"].reshape(BATCH, SEQ, D)
```
